# Optimizing a Trainium2 kernel written in Bass

```python
import numpy as np
import jax
import jax.numpy as jnp

def _softmax(x, axis=-1):
    return jax.nn.softmax(x, axis=axis)

def _gelu(x):
    return jax.nn.gelu(x, approximate=True)

def _silu(x):
    return jax.nn.silu(x)

def _sigmoid(x):
    return jax.nn.sigmoid(x)

def _layernorm(x, axis=-1, eps=1e-05):
    m = jnp.mean(x, axis=axis, keepdims=True)
    v = jnp.var(x, axis=axis, keepdims=True)
    return (x - m) / jnp.sqrt(v + eps)

def _scatter_add(tgt, idx, src, axis=0):
    return tgt.at[idx].add(src)

def _segment_sum(src, seg, n):
    return jax.ops.segment_sum(src, seg, n)
kernel_name = 'mk_decoder_preln_d1_seqx_r4_4e9f67'

def setup_inputs(seed: int=0):
    np.random.seed(seed)
    _w = jnp.asarray

    def _rec_inputs():
        import jax
        import jax.numpy as jnp
        _rk = jax.random.key(seed)
        x = -0.0002928 + 1 * jax.random.normal(jax.random.fold_in(_rk, 1), (32, 256, 256), jnp.float32)
        _lenS = 256 - jax.random.randint(jax.random.fold_in(_rk, 7), (32,), 0, max(1, 256 // 4) + 1, jnp.int32)
        _lenS2 = 256 - jax.random.randint(jax.random.fold_in(_rk, 8), (32,), 0, max(1, 256 // 4) + 1, jnp.int32)
        _ctx_1024P = jax.random.normal(jax.random.fold_in(_rk, 11), (32, 16, 256), jnp.float32)
        _ctx_1024c = jax.random.dirichlet(jax.random.fold_in(_rk, 511), 0.3 * jnp.ones((16,), jnp.float32), (32, 256))
        _ctx_1024t = jnp.einsum('bsk,bkd->bsd', _ctx_1024c, _ctx_1024P)
        _ctx_1024t = _ctx_1024t * jax.lax.rsqrt(jnp.mean(jnp.square(_ctx_1024t)) + 1e-12) * 0.953939
        ctx_1024 = -1.39393e-06 + 0.999914 * (_ctx_1024t + 0.3 * jax.random.normal(jax.random.fold_in(_rk, 611), (32, 256, 256), jnp.float32))
        fside_Bx16xSxS2_0 = 9.80324e-06 + 0.100009 * jax.random.normal(jax.random.fold_in(_rk, 12), (32, 16, 256, 256), jnp.float32)
        fside_SxS2_0 = -2.64403e-05 + 0.100002 * jax.random.normal(jax.random.fold_in(_rk, 14), (256, 256), jnp.float32)
        _validS = jnp.arange(256)[None, :] < _lenS[:, None]
        _validS2 = jnp.arange(256)[None, :] < _lenS2[:, None]
        _causal = jnp.tril(jnp.ones((256, 256), dtype=bool))
        mask_BxS2_bf0 = jnp.logical_not(jnp.ones((32, 256), dtype=bool))
        return (x, ctx_1024, fside_Bx16xSxS2_0, fside_SxS2_0, mask_BxS2_bf0)
    x, ctx_1024, fside_Bx16xSxS2_0, fside_SxS2_0, mask_BxS2_bf0 = _rec_inputs()

    def _L0_attn_setup():
        import jax, jax.numpy as jnp
        import numpy as np
        B, T, E = (4, 512, 256)
        H, D = (8, 128)

        def sinusoidal_pe(length, dim, dtype=jnp.float32):
            pos = jnp.arange(length, dtype=jnp.float32)[:, None]
            inv_freq = jnp.exp(-jnp.log(jnp.float32(10000.0)) * (jnp.arange(0, dim, 2, dtype=jnp.float32) / dim))
            ang = pos * inv_freq[None, :]
            pe = jnp.zeros((length, dim), dtype=jnp.float32)
            pe = pe.at[:, 0::2].set(jnp.sin(ang)).at[:, 1::2].set(jnp.cos(ang))
            return pe.astype(dtype)
        key = jax.random.key(seed)
        kx, kq, kk, kv, ko = jax.random.split(key, 5)
        s = 0.02
        return {'x': jax.random.normal(kx, (B, T, E), dtype=jnp.float32), 'Wq': jax.random.normal(kq, (H * D, E), dtype=jnp.float32) * s, 'Wk': jax.random.normal(kk, (D, E), dtype=jnp.float32) * s, 'Wv': jax.random.normal(kv, (D, E), dtype=jnp.float32) * s, 'Wo': jax.random.normal(ko, (E, H * D), dtype=jnp.float32) * s}
    _L0_attn_all = _L0_attn_setup()
    _L0_attn_in = {k: v for k, v in _L0_attn_all.items() if k in ('Wq', 'Wk', 'Wv', 'Wo')}
    del _L0_attn_all

    def _L0_xattn_setup():
        import jax, jax.numpy as jnp
        import numpy as np
        E = 256
        H = 16
        D = E // H
        key = jax.random.key(seed)
        ks = jax.random.split(key, 12)
        B, T, S = (2, 512, 512)
        inp = {'query': jax.random.normal(ks[0], (B, T, E), jnp.float32), 'key': jax.random.normal(ks[1], (B, S, E), jnp.float32), 'value': jax.random.normal(ks[2], (B, S, E), jnp.float32), 'spatial_bias': jax.random.normal(ks[3], (B, H, T, S), jnp.float32) * 0.1, 'directional_bias': jax.random.normal(ks[4], (B, H, T, S), jnp.float32) * 0.1, 'key_padding_mask': jnp.zeros((B, S), dtype=bool), 'attn_mask': jax.random.normal(ks[5], (T, S), jnp.float32) * 0.1, 'Wq': jax.random.normal(ks[6], (E, E), jnp.float32) / np.sqrt(E), 'bq': jnp.zeros((E,), jnp.float32), 'Wk': jax.random.normal(ks[7], (E, E), jnp.float32) / np.sqrt(E), 'bk': jnp.zeros((E,), jnp.float32), 'Wv': jax.random.normal(ks[8], (E, E), jnp.float32) / np.sqrt(E), 'bv': jnp.zeros((E,), jnp.float32), 'Wo': jax.random.normal(ks[9], (E, E), jnp.float32) / np.sqrt(E), 'bo': jnp.zeros((E,), jnp.float32)}
        return inp
    _L0_xattn_all = _L0_xattn_setup()
    _L0_xattn_in = {k: v for k, v in _L0_xattn_all.items() if k in ('Wq', 'bq', 'Wk', 'bk', 'Wv', 'bv', 'Wo', 'bo')}
    del _L0_xattn_all

    def _L0_ffn_setup():
        import jax, jax.numpy as jnp
        import numpy as np
        E = 8
        K = 2
        D = 256
        H = 256
        B, T = (2, 256)
        key = jax.random.key(seed)
        ks = jax.random.split(key, 6)
        s = 0.02
        return {'x': jax.random.normal(ks[0], (B, T, D), dtype=jnp.float32), 'gate_w': jax.random.normal(ks[1], (E, D), dtype=jnp.float32) * s, 'lb_bias': jnp.zeros((E,), dtype=jnp.float32), 'w1': jax.random.normal(ks[2], (E, H, D), dtype=jnp.float32) * s, 'w2': jax.random.normal(ks[3], (E, D, H), dtype=jnp.float32) * s, 'cfc': jax.random.normal(ks[4], (H, D), dtype=jnp.float32) * s, 'cproj': jax.random.normal(ks[5], (D, H), dtype=jnp.float32) * s}
    _L0_ffn_all = _L0_ffn_setup()
    _L0_ffn_in = {k: v for k, v in _L0_ffn_all.items() if k in ('gate_w', 'lb_bias', 'w1', 'w2', 'cfc', 'cproj')}
    del _L0_ffn_all
    return {'x': x, 'ctx_1024': ctx_1024, 'fside_Bx16xSxS2_0': fside_Bx16xSxS2_0, 'fside_SxS2_0': fside_SxS2_0, 'mask_BxS2_bf0': mask_BxS2_bf0, 'L0_attn_Wq': _L0_attn_in['Wq'], 'L0_attn_Wk': _L0_attn_in['Wk'], 'L0_attn_Wv': _L0_attn_in['Wv'], 'L0_attn_Wo': _L0_attn_in['Wo'], 'L0_xattn_Wq': _L0_xattn_in['Wq'], 'L0_xattn_bq': _L0_xattn_in['bq'], 'L0_xattn_Wk': _L0_xattn_in['Wk'], 'L0_xattn_bk': _L0_xattn_in['bk'], 'L0_xattn_Wv': _L0_xattn_in['Wv'], 'L0_xattn_bv': _L0_xattn_in['bv'], 'L0_xattn_Wo': _L0_xattn_in['Wo'], 'L0_xattn_bo': _L0_xattn_in['bo'], 'L0_ffn_gate_w': _L0_ffn_in['gate_w'], 'L0_ffn_lb_bias': _L0_ffn_in['lb_bias'], 'L0_ffn_w1': _L0_ffn_in['w1'], 'L0_ffn_w2': _L0_ffn_in['w2'], 'L0_ffn_cfc': _L0_ffn_in['cfc'], 'L0_ffn_cproj': _L0_ffn_in['cproj']}

def reference(x, ctx_1024, fside_Bx16xSxS2_0, fside_SxS2_0, mask_BxS2_bf0, L0_attn_Wq, L0_attn_Wk, L0_attn_Wv, L0_attn_Wo, L0_xattn_Wq, L0_xattn_bq, L0_xattn_Wk, L0_xattn_bk, L0_xattn_Wv, L0_xattn_bv, L0_xattn_Wo, L0_xattn_bo, L0_ffn_gate_w, L0_ffn_lb_bias, L0_ffn_w1, L0_ffn_w2, L0_ffn_cfc, L0_ffn_cproj):
    import jax
    import jax.numpy as jnp

    def _L0_attn_ref(x, Wq, Wk, Wv, Wo):
        import jax, jax.numpy as jnp
        import numpy as np
        B, T, E = (4, 512, 256)
        H, D = (8, 128)

        def sinusoidal_pe(length, dim, dtype=jnp.float32):
            pos = jnp.arange(length, dtype=jnp.float32)[:, None]
            inv_freq = jnp.exp(-jnp.log(jnp.float32(10000.0)) * (jnp.arange(0, dim, 2, dtype=jnp.float32) / dim))
            ang = pos * inv_freq[None, :]
            pe = jnp.zeros((length, dim), dtype=jnp.float32)
            pe = pe.at[:, 0::2].set(jnp.sin(ang)).at[:, 1::2].set(jnp.cos(ang))
            return pe.astype(dtype)
        Bv, Tv, Ev = x.shape
        scale = 1.0 / jnp.sqrt(jnp.float32(D)).astype(x.dtype)
        q = (x @ Wq.T).reshape(Bv, Tv, H, D)
        k = (x @ Wk.T).reshape(Bv, Tv, 1, D)
        v = (x @ Wv.T).reshape(Bv, Tv, 1, D)
        k = k + sinusoidal_pe(1, D, k.dtype)
        q = jnp.transpose(q, (0, 2, 1, 3))
        k1 = k[:, :, 0, :]
        v1 = v[:, :, 0, :]
        q = q + sinusoidal_pe(Tv, D, q.dtype)[None, None]
        scores = jnp.einsum('bhtd,bsd->bhts', q, k1) * scale
        causal = jnp.tril(jnp.ones((Tv, Tv), dtype=bool))
        scores = jnp.where(causal[None, None], scores, jnp.finfo(scores.dtype).min)
        probs = jax.nn.softmax(scores, axis=-1)
        attn = jnp.einsum('bhts,bsd->bhtd', probs, v1)
        out = jnp.transpose(attn, (0, 2, 1, 3)).reshape(Bv, Tv, H * D)
        return out @ Wo.T

    def _L0_xattn_ref(query, key, value, spatial_bias, directional_bias, key_padding_mask, attn_mask, Wq, bq, Wk, bk, Wv, bv, Wo, bo):
        import jax, jax.numpy as jnp
        import numpy as np
        E = 256
        H = 16
        D = E // H
        B, T, _ = query.shape
        S = key.shape[1]
        scale = D ** (-0.5)
        q = (query @ Wq.T + bq).reshape(B, T, H, D).transpose(0, 2, 1, 3)
        k = (key @ Wk.T + bk).reshape(B, S, H, D).transpose(0, 2, 1, 3)
        v = (value @ Wv.T + bv).reshape(B, S, H, D).transpose(0, 2, 1, 3)
        scores = jnp.einsum('bhtd,bhsd->bhts', q, k) * scale
        scores = scores + attn_mask[None, None, :, :]
        pad = key_padding_mask[:, None, None, :]
        scores = jnp.where(pad, -jnp.inf, scores)
        if T == S:
            scores = scores + spatial_bias + directional_bias
        probs = jax.nn.softmax(scores, axis=-1)
        out = jnp.einsum('bhts,bhsd->bhtd', probs, v)
        out = out.transpose(0, 2, 1, 3).reshape(B, T, E)
        return out @ Wo.T + bo

    def _L0_ffn_ref(x, gate_w, lb_bias, w1, w2, cfc, cproj):
        import jax, jax.numpy as jnp
        import numpy as np
        E = 8
        K = 2
        D = 256
        H = 256
        B, T = (2, 256)
        Bx, Tx, Dx = x.shape
        logits = jnp.einsum('btd,ed->bte', x, gate_w)
        _, idx = jax.lax.top_k(logits + lb_bias, K)
        sel_logits = jnp.take_along_axis(logits, idx, axis=-1)
        w = jax.nn.sigmoid(sel_logits)
        w = w / (jnp.sum(w, axis=-1, keepdims=True) + 1e-06)
        xf = x.reshape(-1, Dx)
        idxf = idx.reshape(-1, K)
        wf = w.reshape(-1, K)
        onehot = jax.nn.one_hot(idxf, E, dtype=wf.dtype)
        we = jnp.einsum('nke,nk->ne', onehot, wf)
        hidden = jnp.square(jax.nn.relu(jnp.einsum('nd,ehd->neh', xf, w1)))
        expert_out = jnp.einsum('neh,edh->ned', hidden, w2)
        moe_out = jnp.einsum('ned,ne->nd', expert_out, we).reshape(Bx, Tx, Dx)
        sh = jnp.square(jax.nn.relu(jnp.einsum('btd,hd->bth', x, cfc)))
        shared = jnp.einsum('bth,dh->btd', sh, cproj)
        return moe_out + shared
    x = x + _L0_attn_ref(_layernorm(x, axis=-1), L0_attn_Wq, L0_attn_Wk, L0_attn_Wv, L0_attn_Wo)
    x = x + _L0_xattn_ref(_layernorm(x, axis=-1), ctx_1024, ctx_1024, fside_Bx16xSxS2_0, fside_Bx16xSxS2_0, mask_BxS2_bf0, fside_SxS2_0, L0_xattn_Wq, L0_xattn_bq, L0_xattn_Wk, L0_xattn_bk, L0_xattn_Wv, L0_xattn_bv, L0_xattn_Wo, L0_xattn_bo)
    x = x + _L0_ffn_ref(_layernorm(x, axis=-1), L0_ffn_gate_w, L0_ffn_lb_bias, L0_ffn_w1, L0_ffn_w2, L0_ffn_cfc, L0_ffn_cproj)
    return x

_drawn_inputs = setup_inputs


def setup_inputs(seed=0):
    import zlib

    import numpy as np

    out = dict(_drawn_inputs(seed))
    spreads = {'L0_xattn_bq': (0.0, 0.382),
     'L0_xattn_bk': (0.0, 0.8),
     'L0_xattn_bv': (0.0, 0.1),
     'L0_xattn_bo': (0.0, 0.1),
     'L0_ffn_lb_bias': (0.0, 0.571)}
    factors = {'fside_Bx16xSxS2_0': 3.629,
     'fside_SxS2_0': 7.17,
     'L0_attn_Wq': 8.0,
     'L0_attn_Wk': 8.0,
     'L0_ffn_gate_w': 2.682}
    for name, (base, spread) in spreads.items():
        noise = np.random.default_rng([zlib.crc32(name.encode()), seed]).standard_normal(out[name].shape)
        drawn = base * np.exp(spread * noise) if base else spread * noise
        out[name] = jnp.asarray(drawn.astype(out[name].dtype))
    for name, factor in factors.items():
        out[name] = (out[name] * factor).astype(out[name].dtype)
    return out
```

```python
from contextlib import ExitStack

import concourse.bass as bass
from concourse import mybir

F32 = mybir.dt.float32
F16 = mybir.dt.float16
U32 = mybir.dt.uint32
U8 = mybir.dt.uint8
ALU = mybir.AluOpType
ACT = mybir.ActivationFunctionType
AX = mybir.AxisListType

P = 128
BATCHES, T, D = 32, 256, 256
CT = T // P
CD = D // P
AH, AD = 8, 128
BH, BD = 16, 16
NE = 8
NX = NE + 1
HID = 256
PAIRS = BH // 2
DEPTH = 4
SLOTS = 4
W_UP = 64.0
R_UP = 4.0
H_UP = R_UP * R_UP
MASKED = -3.0e38
EPS = 1e-5
A_SCALE = 1.0 / float(AD) ** 0.5
B_HALF = 0.5 / float(BD) ** 0.5

WQ0 = 0
WK0 = WQ0 + CD * AH * AD
WV0 = WK0 + CD * AD
XQ0 = WV0 + CD * AD
XK0 = XQ0 + CD * D
XV0 = XK0 + CD * D
WO0 = XV0 + CD * D
XO0 = WO0 + AH * D
W10 = XO0 + CD * D
W20 = W10 + NX * CD * HID
GT0 = W20 + NX * 2 * D
NW = GT0 + CD * NE
ID0, TRI0, PE0, PC0, IO0 = 0, P, P + 256, P + 512, P + 513
NC = IO0 + NE
STAGE = 1024


def order(text):
    entries = [entry.replace("@", ":").split(":") for entry in text.split()]
    return [(step, int(arg), int(lag)) for step, arg, lag in entries]


ORDERS = {name: order(text) for name, text in dict(
    sync="""
        b_split_q:0@1 b_load:6@2 a_ln:0@1 b_load:7@2 a_T:0@0 b_load:0@1 b_load:1@1 b_load:2@1 b_load:3@1
        b_load:4@1 b_mask:0@1 b_load:5@1 c_f2:8@2""",
    gpsimd="""
        b_comb:0@1 b_comb:1@1 c_ln:0@2 a_ln:0@0 b_comb:2@1 c_f1:0@2 b_ln:0@1 b_split_k:0@1 c_f1:1@2
        b_split_q:0@1 b_comb:3@1 b_comb:4@1 c_f1:2@2 b_comb:5@1 b_comb:6@1 b_kv:0@0 c_f1:3@2 b_comb:7@1
        b_comb:8@1 b_comb:9@1 b_comb:10@1 c_f1:4@2 b_comb:11@1 b_comb:12@1 c_f1:5@2 b_res:0@1 c_f1:6@2
        b_comb:13@1 b_comb:14@1 b_comb:15@1 c_f1:7@2 c_f1:8@2""",
    scalar="""
        a_pt:6@1 a_pv:5@1 a_pv:6@1 a_pt:7@1 c_T:0@2 a_pv:7@1 b_kv:0@1 c_gate:0@2 c_f1:0@2 c_f1:1@2 a_T:0@0
        b_T:0@1 c_f1:2@2 a_kv:0@0 b_q:0@1 b_stack:0@1 b_stack:1@1 b_stack:2@1 b_stack:3@1 b_s:0@1 b_s:1@1
        c_f1:3@2 b_pt:0@1 b_s:2@1 b_s:3@1 b_pt:1@1 b_s:4@1 c_f1:4@2 b_pt:2@1 a_s:0@0 b_s:5@1 a_s:1@0
        b_pt:3@1 b_s:6@1 a_pt:0@0 b_pt:4@1 b_s:7@1 a_s:2@0 c_f1:5@2 b_pt:5@1 b_s:8@1 b_s:9@1 a_pt:1@0
        a_s:3@0 b_pt:6@1 a_pv:0@0 c_f1:6@2 b_pt:7@1 b_s:10@1 a_pt:2@0 b_s:11@1 b_pt:8@1 a_s:4@0 b_pv:7@1
        a_s:5@0 b_s:12@1 a_pv:1@0 b_pt:9@1 c_f1:7@2 a_pt:3@0 b_pt:10@1 b_s:13@1 a_s:6@0 c_f1:8@2 b_pt:11@1
        a_pv:2@0 b_s:14@1 b_pt:12@1 a_pt:4@0 b_s:15@1 b_pt:13@1 a_pv:3@0 a_s:7@0 b_pt:14@1 a_pt:5@0 a_pv:4@0
        b_pt:15@1 b_pv:15@1""",
    vector="""
        a_pv:5@1 b_wo:0@2 c_ln:0@2 a_pv:6@1 a_pt:7@1 b_kv:0@1 c_T:0@2 a_pv:7@1 a_ln:0@0 c_gate:0@2 a_wo:0@1
        b_ln:0@1 a_T:0@0 c_f2:0@2 b_T:0@1 b_stack:4@1 a_kv:0@0 b_stack:5@1 b_stack:6@1 b_stack:7@1 a_q:0@0
        c_f2:1@2 b_s:0@1 a_q:1@0 b_s:1@1 b_n:0@1 a_q:2@0 b_s:2@1 b_n:1@1 b_s:3@1 c_f2:2@2 b_n:2@1 b_s:4@1
        a_q:3@0 b_n:3@1 a_s:0@0 b_s:5@1 b_n:4@1 a_s:1@0 b_s:6@1 a_n:0@0 b_s:7@1 a_s:2@0 b_n:5@1 c_f2:3@2
        b_s:8@1 b_n:6@1 a_n:1@0 a_pt:0@0 a_s:3@0 b_s:9@1 a_n:2@0 b_n:7@1 c_f2:4@2 b_s:10@1 a_pt:1@0 a_s:4@0
        a_n:3@0 b_s:11@1 b_n:8@1 b_n:9@1 a_pv:0@0 a_s:5@0 b_s:12@1 c_f2:5@2 a_pt:2@0 b_n:10@1 b_s:13@1
        a_n:4@0 b_pv:7@1 b_n:11@1 b_n:12@1 a_s:6@0 a_pv:1@0 c_f2:6@2 a_pt:3@0 b_s:14@1 a_n:5@0 b_s:15@1
        b_n:13@1 c_f2:7@2 a_pv:2@0 b_n:14@1 a_pt:4@0 a_s:7@0 b_n:15@1 a_pv:3@0 a_n:6@0 b_mask:0@0 a_pt:5@0
        a_pv:4@0 a_n:7@0 b_pv:15@1 a_pt:6@0 c_f2:8@2""",
    tensor="""
        a_pv:4@1 b_pt:15@2 b_pv:13@2 b_pv:14@2 b_pv:15@2 a_pt:6@1 a_pv:5@1 b_wo:0@2 a_pt:7@1 a_pv:6@1
        b_kv:0@1 c_T:0@2 a_pv:7@1 c_gate:0@2 c_f1:0@2 a_wo:0@1 c_f1:1@2 a_T:0@0 c_f2:0@2 c_f1:2@2 b_T:0@1
        a_kv:0@0 b_stack:4@1 b_q:0@1 b_stack:5@1 b_stack:6@1 c_f2:1@2 b_stack:7@1 a_q:0@0 b_stack:0@1
        b_stack:1@1 b_stack:2@1 b_stack:3@1 a_q:1@0 b_s:0@1 c_f1:3@2 b_s:1@1 a_q:2@0 b_s:2@1 c_f2:2@2
        b_pt:0@1 b_s:3@1 a_q:3@0 b_s:4@1 b_pt:1@1 a_s:0@0 c_f1:4@2 b_s:5@1 b_pv:0@1 b_pt:2@1 a_s:1@0 b_s:6@1
        b_pv:1@1 b_pv:2@1 a_s:2@0 b_s:7@1 b_pt:3@1 c_f2:3@2 a_pt:0@0 b_pt:4@1 b_s:8@1 c_f1:5@2 b_s:9@1
        b_pv:3@1 a_s:3@0 b_pt:5@1 b_pv:4@1 a_pt:1@0 c_f2:4@2 a_s:4@0 b_s:10@1 b_pv:5@1 b_pt:6@1 c_f1:6@2
        a_pv:0@0 b_s:11@1 b_pt:7@1 a_pt:2@0 c_f2:5@2 a_s:5@0 b_s:12@1 b_pv:6@1 b_pv:7@1 b_pt:8@1 c_f1:7@2
        a_s:6@0 b_pt:9@1 b_s:13@1 a_pv:1@0 c_f2:6@2 b_s:14@1 a_pt:3@0 b_pv:8@1 b_pt:10@1 c_f1:8@2 b_pv:9@1
        b_pv:10@1 b_pt:11@1 a_pv:2@0 b_s:15@1 c_f2:7@2 a_pt:4@0 b_pt:12@1 b_pv:11@1 a_s:7@0 a_pv:3@0
        b_pv:12@1 b_pt:13@1 c_f2:8@2 b_pt:14@1 a_pt:5@0""",
).items()}
LAGS = 2


def after(batch, per_batch, n):
    if isinstance(batch, int):
        return max(batch * per_batch + n, 0)
    return batch * per_batch + n


def build(nc, x_d, ctx_d, bias_d, mask_d, pad_d, wpair_d, cst_d, sel_d, bq_d, bk_d, bv_d, bo_d, lb_d, out_d):
    with ExitStack() as ctx:
        def sb(name, shape, dt=F32):
            return ctx.enter_context(nc.sbuf_tensor(name, shape, dt))

        def bank(name):
            return ctx.enter_context(nc.psum_tensor(name, [P, 512], F32))

        def sem(name):
            return ctx.enter_context(nc.semaphore(name))

        wh = sb("w_hi", [P, NW], F16)
        wl = sb("w_lo", [P, NW], F16)
        cst = sb("constants", [P, NC])
        ident = cst[:, ID0:ID0 + P]
        tri = cst[:, TRI0:TRI0 + 256]
        pe_t = cst[:, PE0:PE0 + 256]
        pe_first = cst[:, PC0:PC0 + 1]
        iota = cst[:, IO0:IO0 + NE]
        sel = sb("selectors", [P, 16 * P], F16)
        half_mask = sb("half_mask", [P, CT * T])
        pad = sb("key_padding", [P, T // 4], U32)
        b_mask = sb("b_mask", [P, CT * T])
        bq = sb("bq", [P, CD])
        bq_half = sb("bq_half", [P, CD])
        bk = sb("bk", [P, CD])
        bv = sb("bv", [P, D])
        bo = sb("bo", [P, D])
        lb = sb("lb", [P, NE])
        minus_half = sb("minus_half", [P, CT])
        eps = sb("eps", [P, CT])
        zeros = sb("zeros", [P, CD, T])

        x_ln = sb("x_ln", [P, CT, D])
        x_res = sb("x_res", [P, CT, D])
        x1 = sb("x1", [P, CT, D])
        x1_bo = sb("x1_bo", [P, CT, D])
        x2 = sb("x2", [P, CT, D])
        acc = sb("acc", [P, CT, D])
        ln = {}
        for st in "abc":
            ln[st] = dict(
                stats=sb(f"{st}_stats", [P, CT, 6]), mv=sb(f"{st}_mv", [P, CT, 2]), ve=sb(f"{st}_ve", [P, CT]),
                rstd=sb(f"{st}_rstd", [P, CT]), xn=sb(f"{st}_xn", [P, CT, D]),
                hi=sb(f"{st}_xT_hi", [P, CD, T], F16), lo=sb(f"{st}_xT_lo", [P, CD, T], F16))
        a_k = sb("a_kT", [P, T])
        a_vh = sb("a_v_hi", [P, CT, AD], F16)
        a_vl = sb("a_v_lo", [P, CT, AD], F16)
        a_q = sb("a_qT", [P, AH, T])
        a_t = sb("a_neg_scores", [P, 2, 384])
        a_p = sb("a_probs", [P, DEPTH, 384])
        a_pTh = sb("a_probsT_hi", [P, 2, 384], F16)
        a_pTl = sb("a_probsT_lo", [P, 2, 384], F16)
        a_mx = sb("a_neg_max", [P, 2, CT])
        a_sum = sb("a_sum", [P, DEPTH, CT])
        a_inv = sb("a_inv", [P, DEPTH, CT])
        a_oh = sb("a_oT_hi", [P, AH, T], F16)
        a_ol = sb("a_oT_lo", [P, AH, T], F16)
        ctx_f = sb("ctxT", [P, CD, T])
        ctx_h = sb("ctxT_hi", [P, CD, T], F16)
        ctx_l = sb("ctxT_lo", [P, CD, T], F16)
        b_kf = sb("b_kT", [P, CD, T])
        b_kh = sb("b_kT_hi", [P, CD, T], F16)
        b_kl = sb("b_kT_lo", [P, CD, T], F16)
        b_qf = sb("b_qT", [P, CD, T])
        b_qh = sb("b_qT_hi", [P, CD, T], F16)
        b_ql = sb("b_qT_lo", [P, CD, T], F16)
        q_stack = sb("q_stack", [P, PAIRS, T], F16)
        k_even = sb("k_stack_even", [P, PAIRS, T], F16)
        k_odd = sb("k_stack_odd", [P, PAIRS, T], F16)
        b_v = sb("b_v", [P, CT, BH, 32])
        bias = sb("bias", [P, SLOTS, 2 * CT * T])
        b_t = sb("b_neg_scores", [P, 2, CT, T])
        b_p = sb("b_probs", [P, DEPTH, CT, T])
        b_pT = sb("b_probsT", [P, 2, CT, T])
        b_mx = sb("b_neg_max", [P, 2, CT])
        b_sum = sb("b_sum", [P, DEPTH, CT])
        b_inv = sb("b_inv", [P, DEPTH, CT])
        b_oh = sb("b_oT_hi", [P, CD, T], F16)
        b_ol = sb("b_oT_lo", [P, CD, T], F16)
        c_r = sb("c_relu", [P, 2, 2 * T])
        c_h = sb("c_hidden", [P, 2, 2 * T])
        c_hh = sb("c_hidden_hi", [P, 2, 2 * T], F16)
        c_hl = sb("c_hidden_lo", [P, 2, 2 * T], F16)
        g_lg = sb("g_logits", [P, CT, NE])
        g_sel = sb("g_biased", [P, CT, NE])
        g_top = sb("g_top", [P, CT, 8])
        g_idx = sb("g_idx", [P, CT, 8], U32)
        g_idf = sb("g_idx_f", [P, CT, 2])
        g_m1 = sb("g_mask1", [P, CT, NE])
        g_m2 = sb("g_mask2", [P, CT, NE])
        g_ex = sb("g_exp", [P, CT, NE])
        g_e1 = sb("g_exp1", [P, CT, NE])
        g_sg = sb("g_sigmoid", [P, CT, NE])
        g_w = sb("g_w", [P, CT, NE])
        g_s = sb("g_sum", [P, CT])
        g_s1 = sb("g_sum1", [P, CT])
        g_si = sb("g_inv", [P, CT])
        g_we = sb("g_weights", [P, CT, NE])

        ps_as, ps_apt, ps_am = bank("ps_a_scores"), bank("ps_a_probsT"), bank("ps_a_misc")
        ps_bs, ps_bpt, ps_bm = bank("ps_b_scores"), bank("ps_b_probsT"), bank("ps_b_misc")
        ps_c1, ps_c2 = bank("ps_c_hidden"), bank("ps_c_out")
        ln_bank = {"a": ps_am, "b": ps_bm, "c": ps_c1}

        s_cst = sem("consts_loaded")
        s_stage = [sem(f"stage_loaded{n}") for n in range(SLOTS)]
        s_hi, s_lo, s_sel, s_fix = sem("w_hi_ready"), sem("w_lo_ready"), sem("sel_ready"), sem("pool_setup_ready")
        s_bias = [sem(f"bias_loaded{n}") for n in range(SLOTS)]
        s_xln, s_xres, s_ctx = sem("x_ln_loaded"), sem("x_res_loaded"), sem("ctx_loaded")
        s_out = sem("out_stored")
        s_pad, b_m_ok = sem("pad_loaded"), sem("b_mask_ready")
        s_stat = {st: sem(f"{st}_stats_ready") for st in "abc"}
        s_var = {st: sem(f"{st}_var_ready") for st in "abc"}
        s_ve = {st: sem(f"{st}_var_eps_ready") for st in "abc"}
        s_rstd = {st: sem(f"{st}_rstd_ready") for st in "abc"}
        s_xn = {st: sem(f"{st}_xn_ready") for st in "abc"}
        s_lnT = {st: sem(f"{st}_xT_in_psum") for st in "abc"}
        s_xh = {st: sem(f"{st}_xT_hi_ready") for st in "abc"}
        s_xl = {st: sem(f"{st}_xT_lo_ready") for st in "abc"}
        a_kv_ps, a_kv_ok, a_vl_ok = sem("a_kv_in_psum"), sem("a_kv_ready"), sem("a_v_lo_ready")
        a_q_ps, a_q_ok = sem("a_q_in_psum"), sem("a_q_ready")
        a_s_ps, a_t_ok, a_e_ok = sem("a_scores_in_psum"), sem("a_neg_scores_ready"), sem("a_exp_ready")
        a_i_ok, a_n_ok = sem("a_inv_ready"), sem("a_probs_ready")
        a_pt_ps, a_pth_ok, a_pt_ok = sem("a_probsT_in_psum"), sem("a_probsT_hi_ready"), sem("a_probsT_ready")
        a_pv_ps, a_oh_ok, a_o_ok = sem("a_pv_in_psum"), sem("a_oT_hi_ready"), sem("a_oT_ready")
        a_wo_ps, x1_ok = sem("a_wo_in_psum"), sem("x1_ready")
        b_ch, b_cl = sem("ctx_hi_ready"), sem("ctx_lo_ready")
        b_k_ps, b_kf_ok, b_kh_ok, b_kl_ok = sem("b_k_in_psum"), sem("b_k_ready"), sem("b_k_hi"), sem("b_k_lo")
        b_q_ps, b_qf_ok, b_qh_ok, b_ql_ok = sem("b_q_in_psum"), sem("b_q_ready"), sem("b_q_hi"), sem("b_q_lo")
        b_v_ps, b_v_ok = sem("b_v_in_psum"), sem("b_v_ready")
        b_st_ps = sem("b_stack_in_psum")
        b_qst_ok, b_kst_ok = sem("b_q_stack_ready"), sem("b_k_stack_ready")
        b_c_ok = sem("b_bias_mask_ready")
        b_s_ps, b_t_ok, b_e_ok = sem("b_scores_in_psum"), sem("b_neg_scores_ready"), sem("b_exp_ready")
        b_i_ok, b_n_ok = sem("b_inv_ready"), sem("b_probs_ready")
        b_pt_ps, b_pt_ok = sem("b_probsT_in_psum"), sem("b_probsT_ready")
        b_pv_ps, b_oh_ok, b_o_ok = sem("b_pv_in_psum"), sem("b_oT_hi_ready"), sem("b_oT_ready")
        b_res_ok, b_wo_ps, x2_ok = sem("x1_bo_ready"), sem("b_wo_in_psum"), sem("x2_ready")
        c_g_ps, c_gd, c_ex = sem("c_logits_in_psum"), sem("c_gate_steps"), sem("c_gate_exp")
        c_f1_ps, c_r_ok, c_sq_ok = sem("c_hidden_in_psum"), sem("c_relu_ready"), sem("c_square_ready")
        c_hh_ok, c_h_ok = sem("c_hidden_hi_ready"), sem("c_hidden_ready")
        c_f2_ps, c_a_ok = sem("c_out_in_psum"), sem("c_acc_ready")
        s_carry = sem("carrier")
        GATE_STEPS = 19

        N_PIECES = (NW + STAGE - 1) // STAGE
        pieces = [(n * STAGE, min(NW, (n + 1) * STAGE)) for n in range(N_PIECES)]
        SEL_PIECES = 2
        N_CONST = 7
        FIX = 8

        def carry_waits(eng):
            eng.sem_inc(s_carry, 1)
        NSTG = N_PIECES + SEL_PIECES

        def stage_count(n):
            return 16 * (n // SLOTS + 1)

        def walk(engine, steps, i):
            for name, arg, lag in ORDERS[engine]:
                if isinstance(i, int):
                    if not 0 <= i - lag < BATCHES:
                        continue
                    steps[name](i - lag, arg)
                else:
                    steps[name](i if lag == 0 else i - lag, arg)

        def iterations(eng, engine, steps):
            for i in range(LAGS + 1):
                walk(engine, steps, i)
            with eng.Fori(LAGS + 1, BATCHES - 1) as i:
                walk(engine, steps, i)
            for i in range(BATCHES - 1, BATCHES + LAGS):
                walk(engine, steps, i)

        block = ctx.enter_context(nc.Block())

        @block.sync
        def _(sp):
            sp.dma_start(cst[:, :], cst_d).then_inc(s_cst, 16)
            sp.dma_start(x_ln[:, :, :], x_d[0]).then_inc(s_xln, 16)
            for n in range(NSTG):
                slot = n % SLOTS
                if n >= SLOTS:
                    sp.wait_ge(s_lo, n - SLOTS + 1)
                if n < N_PIECES:
                    a, z = pieces[n]
                    sp.dma_start(bias[:, slot, 0:z - a], wpair_d[:, a:z]).then_inc(s_stage[slot], 16)
                else:
                    a = (n - N_PIECES) * STAGE
                    sp.dma_start(bias[:, slot, :], sel_d[:, a:a + STAGE]).then_inc(s_stage[slot], 16)
            sp.dma_start(bq[:, :], bq_d).then_inc(s_cst, 16)
            sp.dma_start(bk[:, :], bk_d).then_inc(s_cst, 16)
            sp.dma_start(bv[:, :], bv_d).then_inc(s_cst, 16)
            sp.dma_start(bo[:, :], bo_d).then_inc(s_cst, 16)
            sp.dma_start(lb[:, :], lb_d).then_inc(s_cst, 16)
            sp.dma_start(half_mask[:, :], mask_d).then_inc(s_cst, 16)
            sp.wait_ge(s_lo, NSTG)
            for p in range(SLOTS):
                sp.dma_start(bias[:, p, :], bias_d[p]).then_inc(s_bias[p], 16)
            sp.dma_start(ctx_f[:, :, :], ctx_d[0]).then_inc(s_ctx, 16)
            sp.dma_start(pad[:, :], pad_d[0]).then_inc(s_pad, 16)

            def a_ln(b, _):
                sp.wait_ge(x1_ok, after(b, 1, 0))
                sp.dma_start(x_res[:, :, :], x_d[b]).then_inc(s_xres, 16)

            def a_T(b, _):
                sp.wait_ge(s_xn["a"], after(b, 2, 2))
                if not (isinstance(b, int) and b == BATCHES - 1):
                    sp.dma_start(x_ln[:, :, :], x_d[b + 1]).then_inc(s_xln, 16)

            def b_load(b, p):
                sp.wait_ge(b_t_ok, after(b, BH, 2 * p + 2))
                q = p + SLOTS
                if q < PAIRS:
                    sp.dma_start(bias[:, p % SLOTS, :], bias_d[b * PAIRS + q]).then_inc(s_bias[p % SLOTS], 16)
                elif not (isinstance(b, int) and b == BATCHES - 1):
                    sp.dma_start(bias[:, p % SLOTS, :], bias_d[b * PAIRS + q]).then_inc(s_bias[p % SLOTS], 16)

            def b_split_q(b, _):
                if not (isinstance(b, int) and b == BATCHES - 1):
                    sp.wait_ge(b_cl, after(b, 1, 1))
                    sp.dma_start(ctx_f[:, :, :], ctx_d[b + 1]).then_inc(s_ctx, 16)

            def b_mask_row(b, _):
                if not (isinstance(b, int) and b == BATCHES - 1):
                    sp.wait_ge(b_m_ok, after(b, 1, 1))
                    sp.dma_start(pad[:, :], pad_d[b + 1]).then_inc(s_pad, 16)

            def c_f2(b, e):
                if e == NX - 1:
                    sp.wait_ge(c_a_ok, after(b, NX, NX))
                    sp.dma_start(out_d[b], acc[:, :, :]).then_inc(s_out, 16)

            iterations(sp, "sync", dict(a_ln=a_ln, a_T=a_T, b_load=b_load, b_split_q=b_split_q,
                                b_mask=b_mask_row, c_f2=c_f2))
            sp.wait_ge(s_out, 16 * BATCHES)

        @block.gpsimd
        def _(gp):
            gp.memset(minus_half[:, :], -0.5).then_inc(s_fix, 1)
            gp.memset(eps[:, :], EPS).then_inc(s_fix, 1)
            gp.memset(zeros[:, :, :], 0.0).then_inc(s_fix, 1)
            gp.memset(k_even[:, :, :], 0.0).then_inc(s_fix, 1)
            gp.memset(k_odd[:, :, :], 0.0).then_inc(s_fix, 1)
            gp.memset(b_v[:, :, :, :], 0.0).then_inc(s_fix, 1)
            gp.wait_ge(s_cst, 16 * N_CONST)
            gp.tensor_scalar(half_mask[:, :], half_mask[:, :], 0.5, None, ALU.mult).then_inc(s_fix, 1)
            gp.tensor_scalar(bq_half[:, :], bq[:, :], B_HALF, None, ALU.mult).then_inc(s_fix, 1)
            gp.wait_ge(s_fix, FIX)

            def ln_rstd(st):
                def step(b, _):
                    L = ln[st]
                    gp.wait_ge(s_var[st], after(b, 2, 2))
                    gp.tensor_tensor(L["ve"][:, :], L["mv"][:, :, 1], eps[:, :], ALU.add).then_inc(s_ve[st], 1)
                    gp.wait_ge(s_ve[st], after(b, 1, 1))
                    if not isinstance(b, int) or b > 0:
                        gp.wait_ge(s_xn[st], after(b, 2, 0))
                    gp.tensor_tensor(L["rstd"][:, :], L["ve"][:, :], minus_half[:, :], ALU.pow).then_inc(s_rstd[st], 1)
                return step

            def b_kv(b, _):
                gp.wait_ge(s_ctx, after(b, 16, 16))
                gp.wait_ge(b_v_ps, after(b, 1, 0))
                gp.tensor_tensor(ctx_h[:, :, :], ctx_f[:, :, :], zeros[:, :, :], ALU.add).then_inc(b_ch, 1)
                gp.wait_ge(b_ch, after(b, 1, 1))
                gp.tensor_tensor(ctx_l[:, :, :], ctx_f[:, :, :], ctx_h[:, :, :], ALU.subtract).then_inc(b_cl, 1)

            def split(src, hi, lo, src_ok, hi_ok, lo_ok, first, last):
                def step(b, _):
                    gp.wait_ge(src_ok, after(b, 2, 2))
                    gp.wait_ge(b_st_ps, after(b, 8, last - 8))
                    gp.tensor_tensor(hi[:, :, :], src[:, :, :], zeros[:, :, :], ALU.add).then_inc(hi_ok, 1)
                    gp.wait_ge(hi_ok, after(b, 1, 1))
                    gp.tensor_tensor(lo[:, :, :], src[:, :, :], hi[:, :, :], ALU.subtract).then_inc(lo_ok, 1)
                return step

            def b_comb(b, j):
                p = j // 2
                slot = p % SLOTS
                if j == 0:
                    gp.wait_ge(b_m_ok, after(b, 1, 1))
                if j % 2 == 0:
                    gp.wait_ge(s_bias[slot], after(b, 32, 16 * (p // SLOTS + 1)))
                part = bias[:, slot, (j % 2) * 512:(j % 2) * 512 + 512]
                gp.tensor_tensor(part, part, b_mask[:, :], ALU.add).then_inc(b_c_ok, 1)

            def b_res(b, _):
                gp.wait_ge(x1_ok, after(b, 1, 1))
                gp.wait_ge(x2_ok, after(b, 1, 0))
                for c in range(CT):
                    last = gp.tensor_tensor(x1_bo[:, c, :], x1[:, c, :], bo[:, :], ALU.add)
                last.then_inc(b_res_ok, 1)

            def c_f1(b, e):
                u = e % 2
                gp.wait_ge(c_r_ok, after(b, NX, e + 1))
                gp.wait_ge(c_h_ok, after(b, NX, e - 1))
                gp.tensor_tensor(c_h[:, u, :], c_r[:, u, :], c_r[:, u, :], ALU.mult).then_inc(c_sq_ok, 1)
                gp.wait_ge(c_sq_ok, after(b, NX, e + 1))
                gp.wait_ge(c_hh_ok, after(b, NX, e + 1))
                gp.wait_ge(c_f2_ps, after(b, NX, e - 1))
                gp.tensor_tensor(c_hl[:, u, :], c_h[:, u, :], c_hh[:, u, :], ALU.subtract).then_inc(c_h_ok, 1)

            iterations(gp, "gpsimd", dict(a_ln=ln_rstd("a"), b_ln=ln_rstd("b"), c_ln=ln_rstd("c"), b_kv=b_kv,
                                b_split_k=split(b_kf, b_kh, b_kl, b_kf_ok, b_kh_ok, b_kl_ok, 4, 8),
                                b_split_q=split(b_qf, b_qh, b_ql, b_qf_ok, b_qh_ok, b_ql_ok, 0, 8),
                                b_comb=b_comb, b_res=b_res, c_f1=c_f1))

        @block.scalar
        def _(act):
            for n in range(N_PIECES):
                a, z = pieces[n]
                act.wait_ge(s_stage[n % SLOTS], stage_count(n))
                act.activation(wh[:, a:z], bias[:, n % SLOTS, 0:z - a], ACT.Copy, scale=W_UP).then_inc(s_hi, 1)
            act.wait_ge(s_cst, 16 * N_CONST)
            act.wait_ge(s_fix, FIX)

            def ln_hi(st, free_sem, per_batch):
                def step(b, _):
                    L = ln[st]
                    act.wait_ge(s_lnT[st], after(b, 1, 1))
                    act.wait_ge(free_sem, after(b, per_batch, 0))
                    act.activation(L["hi"][:, :, :], ln_bank[st][:, :].rearrange("p (k t) -> p k t", k=CD),
                                   ACT.Copy).then_inc(s_xh[st], 1)
                return step

            def a_kv(b, _):
                act.wait_ge(a_kv_ps, after(b, 1, 1))
                act.wait_ge(a_s_ps, after(b, AH, 0))
                act.activation(a_k[:, :], ps_am[:, 0:T], ACT.Identity, bias=pe_first, scale=1.0 / W_UP).then_inc(a_kv_ok, 1)
                act.wait_ge(a_pv_ps, after(b, AH, 0))
                act.activation(a_vh[:, :, :], ps_am[:, T:2 * T].rearrange("p (c d) -> p c d", c=CT), ACT.Copy,
                               scale=1.0 / W_UP).then_inc(a_kv_ok, 1)

            def a_s(b, h):
                u, d = h % 2, h % DEPTH
                act.wait_ge(a_t_ok, after(b, AH, h + 1))
                act.wait_ge(a_pt_ps, after(b, AH, h - DEPTH + 1))
                act.activation(a_p[:, d, 0:128], a_t[:, u, 0:128], ACT.Exp, bias=a_mx[:, u, 0:1], scale=-1.0,
                               accum_out=a_sum[:, d, 0:1])
                act.activation(a_p[:, d, 128:384], a_t[:, u, 128:384], ACT.Exp, bias=a_mx[:, u, 1:2], scale=-1.0,
                               accum_out=a_sum[:, d, 1:2]).then_inc(a_e_ok, 1)

            def a_pt(b, h):
                act.wait_ge(a_pt_ps, after(b, AH, h + 1))
                act.wait_ge(a_pv_ps, after(b, AH, h - 1))
                act.activation(a_pTh[:, h % 2, :], ps_apt[:, 0:384], ACT.Copy).then_inc(a_pth_ok, 1)

            def a_pv(b, h):
                act.wait_ge(a_pv_ps, after(b, AH, h + 1))
                act.wait_ge(a_wo_ps, after(b, 1, 0))
                act.activation(a_oh[:, h, :], ps_am[:, 0:T], ACT.Copy).then_inc(a_oh_ok, 1)

            def b_kv(b, _):
                act.wait_ge(b_k_ps, after(b, 1, 1))
                act.wait_ge(b_kl_ok, after(b, 1, 0))
                for m in range(CD):
                    act.activation(b_kf[:, m, :], ps_bpt[:, m * T:(m + 1) * T], ACT.Identity, bias=bk[:, m:m + 1],
                                   scale=1.0 / W_UP).then_inc(b_kf_ok, 1)

            def b_q(b, _):
                act.wait_ge(b_q_ps, after(b, 1, 1))
                act.wait_ge(b_ql_ok, after(b, 1, 0))
                for m in range(CD):
                    act.activation(b_qf[:, m, :], ps_bm[:, m * T:(m + 1) * T], ACT.Identity, bias=bq_half[:, m:m + 1],
                                   scale=B_HALF / W_UP).then_inc(b_qf_ok, 1)

            def b_stack(b, r):
                if r >= 4:
                    return
                src = ps_bpt if r % 2 == 0 else ps_bs
                act.wait_ge(b_st_ps, after(b, 8, 4 + r + 1))
                act.wait_ge(b_s_ps, after(b, BH, 0))
                act.activation(q_stack[:, 2 * r:2 * r + 2, :], src[:, :].rearrange("p (q t) -> p q t", q=2),
                               ACT.Copy).then_inc(b_qst_ok, 1)

            def b_s(b, j):
                u, d = j % 2, j % DEPTH
                act.wait_ge(b_t_ok, after(b, BH, j + 1))
                act.wait_ge(b_pt_ps, after(b, BH, j - DEPTH + 1))
                act.activation(b_p[:, d, 0, :], b_t[:, u, 0, :], ACT.Exp, bias=b_mx[:, u, 0:1], scale=-1.0,
                               accum_out=b_sum[:, d, 0:1])
                act.activation(b_p[:, d, 1, :], b_t[:, u, 1, :], ACT.Exp, bias=b_mx[:, u, 1:2], scale=-1.0,
                               accum_out=b_sum[:, d, 1:2]).then_inc(b_e_ok, 1)

            def b_pt(b, j):
                act.wait_ge(b_pt_ps, after(b, BH, j + 1))
                act.wait_ge(b_pv_ps, after(b, BH, j - 1))
                act.activation(b_pT[:, j % 2, :, :], ps_bpt[:, :].rearrange("p (c t) -> p c t", c=CT),
                               ACT.Copy).then_inc(b_pt_ok, 1)

            def b_pv(b, j):
                if j % 8 == 7:
                    act.wait_ge(b_pv_ps, after(b, BH, j + 1))
                    act.wait_ge(b_wo_ps, after(b, 1, 0))
                    act.activation(b_oh[:, j // 8, :], ps_bm[:, 0:T], ACT.Copy).then_inc(b_oh_ok, 1)

            def c_gate(b, _):
                act.wait_ge(c_gd, after(b, GATE_STEPS, 1))
                act.wait_ge(c_gd, after(b, GATE_STEPS, 0))
                act.activation(g_ex[:, :, :], g_lg[:, :, :], ACT.Exp, scale=-1.0).then_inc(c_ex, 1)

            def c_f1(b, e):
                act.wait_ge(c_f1_ps, after(b, NX, e + 1))
                act.wait_ge(c_sq_ok, after(b, NX, e - 1))
                act.activation(c_r[:, e % 2, :], ps_c1[:, :], ACT.Relu, scale=R_UP / W_UP).then_inc(c_r_ok, 1)
                act.wait_ge(c_r_ok, after(b, NX, e + 1))
                act.wait_ge(c_f2_ps, after(b, NX, e - 1))
                act.activation(c_hh[:, e % 2, :], c_r[:, e % 2, :], ACT.Square).then_inc(c_hh_ok, 1)

            iterations(act, "scalar", dict(a_T=ln_hi("a", a_q_ps, 4), b_T=ln_hi("b", b_q_ps, 1), c_T=ln_hi("c", c_f1_ps, NX),
                                 a_kv=a_kv, a_s=a_s, a_pt=a_pt, a_pv=a_pv, b_kv=b_kv, b_q=b_q, b_stack=b_stack,
                                 b_s=b_s, b_pt=b_pt, b_pv=b_pv, c_gate=c_gate, c_f1=c_f1))

        @block.vector
        def _(dve):
            for n in range(NSTG):
                if n < N_PIECES:
                    dve.wait_ge(s_hi, n + 1)
                    a, z = pieces[n]
                    dve.scalar_tensor_tensor(out=wl[:, a:z], in0=bias[:, n % SLOTS, 0:z - a], scalar=W_UP,
                                             in1=wh[:, a:z], op0=ALU.mult, op1=ALU.subtract).then_inc(s_lo, 1)
                else:
                    dve.wait_ge(s_stage[n % SLOTS], stage_count(n))
                    a = (n - N_PIECES) * STAGE
                    dve.tensor_copy(sel[:, a:a + STAGE], bias[:, n % SLOTS, :]).then_inc(s_lo, 1)
            dve.wait_ge(s_lo, NSTG)
            dve.wait_ge(s_cst, 16 * N_CONST)
            dve.wait_ge(s_fix, FIX)

            def ln_stats(st, x, x_ok, x_count):
                def step(b, _):
                    L = ln[st]
                    dve.wait_ge(x_ok, after(b, x_count, x_count))
                    for c in range(CT):
                        dve.bn_stats(L["stats"][:, c, :], x[:, c, :]).then_inc(s_stat[st], 1)
                    dve.wait_ge(s_stat[st], after(b, 2, 2))
                    carry_waits(dve)
                    for c in range(CT):
                        dve.bn_aggr(L["mv"][:, c, :], L["stats"][:, c, :]).then_inc(s_var[st], 1)
                    dve.wait_ge(s_rstd[st], after(b, 1, 1))
                    dve.wait_ge(s_lnT[st], after(b, 1, 0))
                    for c in range(CT):
                        dve.tensor_scalar(L["xn"][:, c, :], x[:, c, :], L["mv"][:, c, 0:1], L["rstd"][:, c:c + 1],
                                          ALU.subtract, ALU.mult).then_inc(s_xn[st], 1)
                return step

            def ln_lo(st):
                def step(b, _):
                    L = ln[st]
                    dve.wait_ge(s_xh[st], after(b, 1, 1))
                    dve.tensor_tensor(L["lo"][:, :, :], ln_bank[st][:, :].rearrange("p (k t) -> p k t", k=CD),
                                      L["hi"][:, :, :], ALU.subtract).then_inc(s_xl[st], 1)
                return step

            def a_wo(b, _):
                dve.wait_ge(a_wo_ps, after(b, 1, 1))
                dve.wait_ge(s_xres, after(b, 16, 16))
                dve.wait_ge(b_res_ok, after(b, 1, 0))
                dve.scalar_tensor_tensor(out=x1[:, :, :], in0=ps_am[:, :].rearrange("p (c d) -> p c d", c=CT),
                                         scalar=1.0 / W_UP, in1=x_res[:, :, :], op0=ALU.mult,
                                         op1=ALU.add).then_inc(x1_ok, 1)

            def a_kv(b, _):
                dve.wait_ge(a_kv_ok, after(b, 2, 2))
                dve.wait_ge(a_pv_ps, after(b, AH, 0))
                dve.scalar_tensor_tensor(out=a_vl[:, :, :], in0=ps_am[:, T:2 * T].rearrange("p (c d) -> p c d", c=CT),
                                         scalar=1.0 / W_UP, in1=a_vh[:, :, :], op0=ALU.mult,
                                         op1=ALU.subtract).then_inc(a_vl_ok, 1)

            def a_pt(b, h):
                dve.wait_ge(a_pth_ok, after(b, AH, h + 1))
                dve.wait_ge(a_pv_ps, after(b, AH, h - 1))
                dve.tensor_tensor(a_pTl[:, h % 2, :], ps_apt[:, 0:384], a_pTh[:, h % 2, :],
                                  ALU.subtract).then_inc(a_pt_ok, 1)

            def a_pv(b, h):
                dve.wait_ge(a_oh_ok, after(b, AH, h + 1))
                dve.wait_ge(a_wo_ps, after(b, 1, 0))
                dve.tensor_tensor(a_ol[:, h, :], ps_am[:, 0:T], a_oh[:, h, :], ALU.subtract).then_inc(a_o_ok, 1)

            def a_qp(b, r):
                dve.wait_ge(a_q_ps, after(b, 4, r + 1))
                dve.wait_ge(a_s_ps, after(b, AH, 0))
                for n in range(2):
                    last = dve.scalar_tensor_tensor(out=a_q[:, 2 * r + n, :], in0=ps_am[:, n * T:(n + 1) * T],
                                                    scalar=1.0 / W_UP, in1=pe_t, op0=ALU.mult, op1=ALU.add)
                last.then_inc(a_q_ok, 1)

            def a_s(b, h):
                u = h % 2
                dve.wait_ge(a_s_ps, after(b, AH, h + 1))
                dve.wait_ge(a_e_ok, after(b, AH, h - 1))
                carry_waits(dve)
                dve.tensor_tensor_reduce(out=a_t[:, u, 0:128], in0=ps_as[:, 0:128], in1=tri[:, 128:256], scale=-A_SCALE,
                                         scalar=3.0e38, op0=ALU.add, op1=ALU.min, accum_out=a_mx[:, u, 0:1])
                dve.tensor_tensor_reduce(out=a_t[:, u, 128:384], in0=ps_as[:, 128:384], in1=tri, scale=-A_SCALE,
                                         scalar=3.0e38, op0=ALU.add, op1=ALU.min,
                                         accum_out=a_mx[:, u, 1:2]).then_inc(a_t_ok, 1)

            def a_n(b, h):
                u = h % DEPTH
                dve.wait_ge(a_e_ok, after(b, AH, h + 1))
                dve.reciprocal(a_inv[:, u, :], a_sum[:, u, :]).then_inc(a_i_ok, 1)
                dve.wait_ge(a_i_ok, after(b, AH, h + 1))
                dve.tensor_scalar(a_p[:, u, 0:128], a_p[:, u, 0:128], a_inv[:, u, 0:1], None, ALU.mult)
                dve.tensor_scalar(a_p[:, u, 128:384], a_p[:, u, 128:384], a_inv[:, u, 1:2], None,
                                  ALU.mult).then_inc(a_n_ok, 1)

            def b_kv(b, _):
                dve.wait_ge(b_v_ps, after(b, 1, 1))
                dve.wait_ge(b_pv_ps, after(b, BH, 0))
                for c in range(CT):
                    for r in range(2):
                        v = ps_bs[:, c * D:(c + 1) * D].rearrange("p (h r d) -> p r h d", r=2, d=BD)[:, r]
                        last = dve.scalar_tensor_tensor(out=b_v[:, c, r:BH:2, r * BD:(r + 1) * BD], in0=v,
                                                        scalar=1.0 / W_UP, in1=bv[:, :].rearrange(
                                                            "p (h r d) -> p r h d", r=2, d=BD)[:, r],
                                                        op0=ALU.mult, op1=ALU.add)
                    last.then_inc(b_v_ok, 1)

            def b_mask_row(b, _):
                dve.wait_ge(s_pad, after(b, 16, 16))
                dve.wait_ge(b_c_ok, after(b, BH, 0))
                for c in range(CT):
                    last = dve.scalar_tensor_tensor(out=b_mask[:, c * T:(c + 1) * T], in0=pad[:, :].bitcast(U8), scalar=MASKED,
                                                    in1=half_mask[:, c * T:(c + 1) * T], op0=ALU.mult, op1=ALU.add)
                last.then_inc(b_m_ok, 1)

            def b_stack(b, r):
                if r < 4:
                    return
                q = r - 4
                src = ps_bpt if r % 2 == 0 else ps_bs
                dve.wait_ge(b_st_ps, after(b, 8, q + 1))
                dve.wait_ge(b_s_ps, after(b, BH, 0))
                dve.tensor_copy(k_even[0:64, 2 * q:2 * q + 2, :], src[0:64, :].rearrange("p (q t) -> p q t", q=2))
                dve.tensor_copy(k_odd[64:128, 2 * q:2 * q + 2, :],
                                src[64:128, :].rearrange("p (q t) -> p q t", q=2)).then_inc(b_kst_ok, 1)

            def b_s(b, j):
                u = j % 2
                slot = (j // 2) % SLOTS
                dve.wait_ge(b_s_ps, after(b, BH, j + 1))
                dve.wait_ge(b_c_ok, after(b, BH, j + 1))
                dve.wait_ge(b_e_ok, after(b, BH, j - 1))
                carry_waits(dve)
                for c in range(CT):
                    at = (j % 2) * 512 + c * T
                    last = dve.tensor_tensor_reduce(out=b_t[:, u, c, :], in0=ps_bs[:, c * T:(c + 1) * T],
                                                    in1=bias[:, slot, at:at + T], scale=-2.0, scalar=3.0e38,
                                                    op0=ALU.add, op1=ALU.min, accum_out=b_mx[:, u, c:c + 1])
                last.then_inc(b_t_ok, 1)

            def b_n(b, j):
                u = j % DEPTH
                dve.wait_ge(b_e_ok, after(b, BH, j + 1))
                dve.reciprocal(b_inv[:, u, :], b_sum[:, u, :]).then_inc(b_i_ok, 1)
                dve.wait_ge(b_i_ok, after(b, BH, j + 1))
                for c in range(CT):
                    last = dve.tensor_scalar(b_p[:, u, c, :], b_p[:, u, c, :], b_inv[:, u, c:c + 1], None, ALU.mult)
                last.then_inc(b_n_ok, 1)

            def b_pv(b, j):
                if j % 8 == 7:
                    dve.wait_ge(b_oh_ok, after(b, 2, j // 8 + 1))
                    dve.wait_ge(b_wo_ps, after(b, 1, 0))
                    dve.tensor_tensor(b_ol[:, j // 8, :], ps_bm[:, 0:T], b_oh[:, j // 8, :],
                                      ALU.subtract).then_inc(b_o_ok, 1)

            def b_wo(b, _):
                dve.wait_ge(b_wo_ps, after(b, 1, 1))
                dve.wait_ge(b_res_ok, after(b, 1, 1))
                dve.wait_ge(c_a_ok, after(b, NX, 0))
                dve.scalar_tensor_tensor(out=x2[:, :, :], in0=ps_bm[:, :].rearrange("p (c d) -> p c d", c=CT),
                                         scalar=1.0 / W_UP, in1=x1_bo[:, :, :], op0=ALU.mult,
                                         op1=ALU.add).then_inc(x2_ok, 1)

            def c_gate(b, _):
                G = GATE_STEPS
                dve.wait_ge(c_g_ps, after(b, 1, 1))
                dve.wait_ge(c_gd, after(b, G, 0))
                dve.tensor_scalar(g_lg[:, :, :], ps_c2[:, 0:CT * NE].rearrange("p (c e) -> p c e", c=CT), 1.0 / W_UP,
                                  None, ALU.mult).then_inc(c_gd, 1)
                dve.wait_ge(c_gd, after(b, G, 1))
                for c in range(CT):
                    dve.tensor_tensor(g_sel[:, c, :], g_lg[:, c, :], lb[:, :], ALU.add).then_inc(c_gd, 1)
                dve.wait_ge(c_gd, after(b, G, 3))
                carry_waits(dve)
                for c in range(CT):
                    dve.max(g_top[:, c, :], g_sel[:, c, :]).then_inc(c_gd, 1)
                dve.wait_ge(c_gd, after(b, G, 5))
                carry_waits(dve)
                for c in range(CT):
                    dve.max_index(g_idx[:, c, :], g_top[:, c, :], g_sel[:, c, :]).then_inc(c_gd, 1)
                dve.wait_ge(c_ex, after(b, 1, 1))
                dve.tensor_scalar(g_e1[:, :, :], g_ex[:, :, :], 1.0, None, ALU.add).then_inc(c_gd, 1)
                dve.wait_ge(c_gd, after(b, G, 8))
                dve.tensor_copy(g_idf[:, :, :], g_idx[:, :, 0:2]).then_inc(c_gd, 1)
                dve.reciprocal(g_sg[:, :, :], g_e1[:, :, :]).then_inc(c_gd, 1)
                dve.wait_ge(c_gd, after(b, G, 10))
                for c in range(CT):
                    dve.tensor_scalar(g_m1[:, c, :], iota, g_idf[:, c, 0:1], None, ALU.is_equal).then_inc(c_gd, 1)
                dve.wait_ge(c_gd, after(b, G, 12))
                for c in range(CT):
                    dve.scalar_tensor_tensor(out=g_m2[:, c, :], in0=iota, scalar=g_idf[:, c, 1:2], in1=g_m1[:, c, :],
                                             op0=ALU.is_equal, op1=ALU.add).then_inc(c_gd, 1)
                dve.wait_ge(c_gd, after(b, G, 14))
                dve.tensor_tensor(g_w[:, :, :], g_m2[:, :, :], g_sg[:, :, :], ALU.mult).then_inc(c_gd, 1)
                dve.wait_ge(c_gd, after(b, G, 15))
                dve.reduce_sum(g_s[:, :], g_w[:, :, :], axis=AX.X).then_inc(c_gd, 1)
                dve.wait_ge(c_gd, after(b, G, 16))
                dve.tensor_scalar(g_s1[:, :], g_s[:, :], 1e-6, None, ALU.add).then_inc(c_gd, 1)
                dve.wait_ge(c_gd, after(b, G, 17))
                dve.reciprocal(g_si[:, :], g_s1[:, :]).then_inc(c_gd, 1)
                dve.wait_ge(c_gd, after(b, G, 18))
                for c in range(CT):
                    last = dve.tensor_scalar(g_we[:, c, :], g_w[:, c, :], g_si[:, c:c + 1], 1.0 / (W_UP * H_UP),
                                             ALU.mult, ALU.mult)
                last.then_inc(c_gd, 1)

            def c_f2(b, e):
                dve.wait_ge(c_f2_ps, after(b, NX, e + 1))
                if e == 0:
                    dve.wait_ge(s_out, after(b, 16, 0))
                    dve.scalar_tensor_tensor(out=acc[:, :, :], in0=ps_c2[:, :].rearrange("p (c d) -> p c d", c=CT),
                                             scalar=1.0 / (W_UP * H_UP), in1=x2[:, :, :], op0=ALU.mult,
                                             op1=ALU.add).then_inc(c_a_ok, 1)
                    return
                dve.wait_ge(c_a_ok, after(b, NX, e))
                for c in range(CT):
                    last = dve.scalar_tensor_tensor(out=acc[:, c, :], in0=ps_c2[:, c * D:(c + 1) * D],
                                                    scalar=g_we[:, c, e - 1:e], in1=acc[:, c, :],
                                                    op0=ALU.mult, op1=ALU.add)
                last.then_inc(c_a_ok, 1)

            iterations(dve, "vector", dict(a_ln=ln_stats("a", x_ln, s_xln, 16), b_ln=ln_stats("b", x1, x1_ok, 1),
                                 c_ln=ln_stats("c", x2, x2_ok, 1), a_T=ln_lo("a"), b_T=ln_lo("b"), c_T=ln_lo("c"),
                                 a_wo=a_wo, a_kv=a_kv, a_pt=a_pt, a_pv=a_pv, a_q=a_qp, a_s=a_s, a_n=a_n, b_kv=b_kv, b_mask=b_mask_row,
                                 b_stack=b_stack, b_s=b_s, b_n=b_n,
                                 b_pv=b_pv, b_wo=b_wo, c_gate=c_gate, c_f2=c_f2))

        @block.tensor
        def _(pe):
            pe.wait_ge(s_lo, NSTG)
            pe.wait_ge(s_cst, 16 * N_CONST)
            pe.wait_ge(s_fix, FIX)

            def pair_product(out, stat, mov, full=False, chunks=CD):
                parts = [("h", "h"), ("h", "l"), ("l", "h")] + ([("l", "l")] if full else [])
                for k in range(chunks):
                    for n, (s, m) in enumerate(parts):
                        last = pe.matmul(out, stat(s, k), mov(m, k), start=(k == 0 and n == 0),
                                         stop=(k == chunks - 1 and n == len(parts) - 1))
                return last

            def w(part, at, width):
                return (wh if part == "h" else wl)[:, at:at + width]

            def tokens(st):
                L = ln[st]
                return lambda part, k, c0=0, n=T: (L["hi"] if part == "h" else L["lo"])[:, k, c0:c0 + n]

            def context(part, k, c0=0, n=T):
                return (ctx_h if part == "h" else ctx_l)[:, k, c0:c0 + n]

            def ln_T(st, free_sem, per_batch):
                def step(b, _):
                    L = ln[st]
                    pe.wait_ge(s_xn[st], after(b, 2, 2))
                    pe.wait_ge(free_sem, after(b, per_batch, 0))
                    for k in range(CD):
                        for c in range(CT):
                            last = pe.transpose(ln_bank[st][:, k * T + c * P:k * T + (c + 1) * P],
                                                L["xn"][:, c, k * P:(k + 1) * P], ident)
                    last.then_inc(s_lnT[st], 1)
                return step

            ta, tb, tc = tokens("a"), tokens("b"), tokens("c")

            def a_kv(b, _):
                pe.wait_ge(s_xl["a"], after(b, 1, 1))
                pair_product(ps_am[:, 0:T], lambda s, k: w(s, WK0 + k * AD, AD), lambda m, k: ta(m, k))
                for c in range(CT):
                    last = pair_product(ps_am[:, T + c * AD:T + (c + 1) * AD], lambda s, k: ta(s, k, c * P, P),
                                        lambda m, k: w(m, WV0 + k * AD, AD))
                last.then_inc(a_kv_ps, 1)

            def a_qp(b, r):
                if r == 0:
                    pe.wait_ge(a_vl_ok, after(b, 1, 1))
                else:
                    pe.wait_ge(a_q_ok, after(b, 4, r))
                for n in range(2):
                    h = 2 * r + n
                    last = pair_product(ps_am[:, n * T:(n + 1) * T],
                                        lambda s, k: w(s, WQ0 + k * AH * AD + h * AD, AD), lambda m, k: ta(m, k))
                last.then_inc(a_q_ps, 1)

            def a_s(b, h):
                pe.wait_ge(a_q_ok, after(b, 4, h // 2 + 1))
                pe.wait_ge(a_t_ok, after(b, AH, h))
                pe.matmul(ps_as[:, 0:128], a_q[:, h, 0:P], a_k[:, 0:P], start=True, stop=True)
                pe.matmul(ps_as[:, 128:384], a_q[:, h, P:T], a_k[:, :], start=True, stop=True).then_inc(a_s_ps, 1)

            def a_pt(b, h):
                u = h % DEPTH
                pe.wait_ge(a_n_ok, after(b, AH, h + 1))
                pe.wait_ge(a_pt_ok, after(b, AH, h))
                pe.transpose(ps_apt[:, 0:128], a_p[:, u, 0:128], ident)
                pe.transpose(ps_apt[:, 128:256], a_p[:, u, 128:256], ident)
                pe.transpose(ps_apt[:, 256:384], a_p[:, u, 256:384], ident).then_inc(a_pt_ps, 1)

            def a_pv(b, h):
                u = h % 2
                pe.wait_ge(a_pt_ok, after(b, AH, h + 1))
                if h == 0:
                    pe.wait_ge(a_q_ok, after(b, 4, 4))
                else:
                    pe.wait_ge(a_o_ok, after(b, AH, h))
                for n, (v, pT) in enumerate([(a_vh, a_pTh), (a_vh, a_pTl), (a_vl, a_pTh)]):
                    pe.matmul(ps_am[:, 0:T], v[:, 0, :], pT[:, u, 0:T], start=(n == 0), stop=False)
                    last = pe.matmul(ps_am[:, P:T], v[:, 1, :], pT[:, u, T:384], start=False, stop=(n == 2))
                last.then_inc(a_pv_ps, 1)

            def a_wo(b, _):
                pe.wait_ge(a_o_ok, after(b, AH, AH))
                for c in range(CT):
                    last = pair_product(ps_am[:, c * D:(c + 1) * D],
                                        lambda s, h: (a_oh if s == "h" else a_ol)[:, h, c * P:(c + 1) * P],
                                        lambda m, h: w(m, WO0 + h * D, D), chunks=AH)
                last.then_inc(a_wo_ps, 1)

            def b_kv(b, _):
                pe.wait_ge(b_cl, after(b, 1, 1))
                pe.wait_ge(b_pt_ok, after(b, BH, 0))
                for m in range(CD):
                    last = pair_product(ps_bpt[:, m * T:(m + 1) * T], lambda s, k: w(s, XK0 + k * D + m * P, P),
                                        lambda mm, k: context(mm, k))
                last.then_inc(b_k_ps, 1)
                pe.wait_ge(b_t_ok, after(b, BH, 0))
                for c in range(CT):
                    last = pair_product(ps_bs[:, c * D:(c + 1) * D], lambda s, k: context(s, k, c * P, P),
                                        lambda mm, k: w(mm, XV0 + k * D, D))
                last.then_inc(b_v_ps, 1)

            def b_q(b, _):
                pe.wait_ge(s_xl["b"], after(b, 1, 1))
                for m in range(CD):
                    last = pair_product(ps_bm[:, m * T:(m + 1) * T], lambda s, k: w(s, XQ0 + k * D + m * P, P),
                                        lambda mm, k: tb(mm, k))
                last.then_inc(b_q_ps, 1)

            def b_stack(b, r):
                dst = ps_bpt if r % 2 == 0 else ps_bs
                q = r % 4
                if r >= 4:
                    pe.wait_ge(b_kl_ok, after(b, 1, 1))
                    if r == 4:
                        pe.wait_ge(b_kf_ok, after(b, 2, 2))
                    elif r == 5:
                        pe.wait_ge(b_v_ok, after(b, 2, 2))
                    else:
                        pe.wait_ge(b_kst_ok, after(b, 4, q - 1))
                    hi, lo, at = b_kh, b_kl, 8
                else:
                    pe.wait_ge(b_ql_ok, after(b, 1, 1))
                    if r < 2:
                        pe.wait_ge(b_kst_ok, after(b, 4, r + 3))
                    else:
                        pe.wait_ge(b_qst_ok, after(b, 4, r - 1))
                    hi, lo, at = b_qh, b_ql, 0
                for n in range(2):
                    pair = 2 * q + n
                    m, row = pair // 4, pair % 4
                    pe.matmul(dst[:, n * T:(n + 1) * T], sel[:, (at + row) * P:(at + row + 1) * P], hi[:, m, :],
                              start=True, stop=False)
                    last = pe.matmul(dst[:, n * T:(n + 1) * T], sel[:, (at + 4 + row) * P:(at + 5 + row) * P], lo[:, m, :],
                                     start=False, stop=True)
                last.then_inc(b_st_ps, 1)

            def b_s(b, j):
                if j == 0:
                    pe.wait_ge(b_qst_ok, after(b, 4, 4))
                    pe.wait_ge(b_kst_ok, after(b, 4, 4))
                else:
                    pe.wait_ge(b_t_ok, after(b, BH, j))
                k = k_even if j % 2 == 0 else k_odd
                for c in range(CT):
                    last = pe.matmul(ps_bs[:, c * T:(c + 1) * T], q_stack[:, j // 2, c * P:(c + 1) * P], k[:, j // 2, :],
                                     start=True, stop=True)
                last.then_inc(b_s_ps, 1)

            def b_pt(b, j):
                u = j % DEPTH
                pe.wait_ge(b_n_ok, after(b, BH, j + 1))
                if j > 0:
                    pe.wait_ge(b_pt_ok, after(b, BH, j))
                for s in range(CT):
                    for c in range(CT):
                        last = pe.transpose(ps_bpt[:, s * T + c * P:s * T + (c + 1) * P],
                                            b_p[:, u, c, s * P:(s + 1) * P], ident)
                last.then_inc(b_pt_ps, 1)

            def b_pv(b, j):
                u, row = j % 2, 32 * (j % 8 // 2)
                pe.wait_ge(b_pt_ok, after(b, BH, j + 1))
                if j == 0:
                    pe.wait_ge(b_qf_ok, after(b, 2, 2))
                    pe.wait_ge(b_v_ok, after(b, 2, 2))
                elif j % 8 == 0:
                    pe.wait_ge(b_o_ok, after(b, 2, j // 8))
                for s in range(CT):
                    last = pe.matmul(ps_bm[row:row + 32, 0:T], b_v[:, s, j, :], b_pT[:, u, s, :],
                                     start=(s == 0 and j % 2 == 0), stop=(s == CT - 1 and j % 2 == 1))
                last.then_inc(b_pv_ps, 1)

            def b_wo(b, _):
                pe.wait_ge(b_o_ok, after(b, 2, 2))
                for c in range(CT):
                    last = pair_product(ps_bm[:, c * D:(c + 1) * D],
                                        lambda s, g: (b_oh if s == "h" else b_ol)[:, g, c * P:(c + 1) * P],
                                        lambda m, g: w(m, XO0 + g * D, D))
                last.then_inc(b_wo_ps, 1)

            def c_gate(b, _):
                pe.wait_ge(s_xl["c"], after(b, 1, 1))
                pe.wait_ge(c_a_ok, after(b, NX, 0))
                for c in range(CT):
                    last = pair_product(ps_c2[:, c * NE:(c + 1) * NE], lambda s, k: tc(s, k, c * P, P),
                                        lambda m, k: w(m, GT0 + k * NE, NE), full=True)
                last.then_inc(c_g_ps, 1)

            def c_f1(b, e):
                if e == 0:
                    pe.wait_ge(s_xl["c"], after(b, 1, 1))
                else:
                    pe.wait_ge(c_r_ok, after(b, NX, e))
                for m in range(2):
                    last = pair_product(ps_c1[:, m * T:(m + 1) * T],
                                        lambda s, k: w(s, W10 + (e * CD + k) * HID + m * P, P), lambda mm, k: tc(mm, k))
                last.then_inc(c_f1_ps, 1)

            def c_f2(b, e):
                pe.wait_ge(c_h_ok, after(b, NX, e + 1))
                if e == 0:
                    pe.wait_ge(c_gd, after(b, GATE_STEPS, 1))
                else:
                    pe.wait_ge(c_a_ok, after(b, NX, e))
                for c in range(CT):
                    last = pair_product(ps_c2[:, c * D:(c + 1) * D],
                                        lambda s, m: (c_hh if s == "h" else c_hl)[:, e % 2,
                                                                                  m * T + c * P:m * T + (c + 1) * P],
                                        lambda mm, m: w(mm, W20 + (e * 2 + m) * D, D))
                last.then_inc(c_f2_ps, 1)

            iterations(pe, "tensor", dict(a_T=ln_T("a", x1_ok, 1), b_T=ln_T("b", x2_ok, 1), c_T=ln_T("c", c_r_ok, NX),
                                a_kv=a_kv, a_q=a_qp, a_s=a_s, a_pt=a_pt, a_pv=a_pv, a_wo=a_wo, b_kv=b_kv, b_q=b_q,
                                b_stack=b_stack, b_s=b_s, b_pt=b_pt, b_pv=b_pv, b_wo=b_wo, c_gate=c_gate, c_f1=c_f1,
                                c_f2=c_f2))


def constants():
    import numpy as np
    cst = np.zeros((P, NC), np.float32)
    cst[:, ID0:ID0 + P] = np.eye(P, dtype=np.float32)
    cst[:, TRI0 + P:TRI0 + 2 * P] = np.where(np.tril(np.ones((P, P), bool)), 0.0, -1e30)
    pos = np.arange(T, dtype=np.float32)[:, None]
    inv = np.exp(-np.log(np.float32(10000.0)) * (np.arange(0, AD, 2, dtype=np.float32) / np.float32(AD))).astype(np.float32)
    ang = pos * inv[None, :]
    table = np.zeros((T, AD), np.float32)
    table[:, 0::2] = np.sin(ang)
    table[:, 1::2] = np.cos(ang)
    cst[:, PE0:PE0 + T] = table.T
    cst[:, PC0] = table[0]
    cst[:, IO0:IO0 + NE] = np.arange(NE, dtype=np.float32)
    sel = np.zeros((P, 16, P), np.float32)
    for kind, rows in enumerate([(0, 1), (2, 3), (0, 2), (1, 3)]):
        for row in range(4):
            for head in range(2):
                for r in rows:
                    for d in range(BD):
                        sel[32 * row + BD * head + d, 4 * kind + row, 64 * head + BD * r + d] = 1.0
    return cst, sel.reshape(P, 16 * P)


def kernel(**inputs):
    import numpy as np
    import concourse.bacc as bacc
    from concourse.bass_utils import run_bass_kernel_spmd

    a = {k: np.asarray(v) for k, v in inputs.items()}

    def chunks(m):
        return m.reshape(-1, P, m.shape[1]).transpose(1, 0, 2).reshape(P, -1)

    wpair = [chunks(a["L0_attn_Wq"].T), chunks(a["L0_attn_Wk"].T), chunks(a["L0_attn_Wv"].T),
             chunks(a["L0_xattn_Wq"].T), chunks(a["L0_xattn_Wk"].T), chunks(a["L0_xattn_Wv"].T),
             chunks(a["L0_attn_Wo"].T), chunks(a["L0_xattn_Wo"].T), chunks(a["L0_ffn_cfc"].T)]
    wpair += [chunks(a["L0_ffn_w1"][e].T) for e in range(NE)]
    wpair += [chunks(a["L0_ffn_cproj"].T)] + [chunks(a["L0_ffn_w2"][e].T) for e in range(NE)]
    wpair += [chunks(a["L0_ffn_gate_w"].T)]
    cst, sel = constants()

    def rows(m):
        return m.reshape(-1, CT, P, m.shape[-1]).transpose(0, 2, 1, 3)

    arrays = {
        "x": rows(a["x"]),
        "ctx": rows(a["ctx_1024"].transpose(0, 2, 1)),
        "bias": a["fside_Bx16xSxS2_0"].reshape(BATCHES * PAIRS, 2 * CT, P, T).transpose(0, 2, 1, 3).reshape(
            BATCHES * PAIRS, P, 2 * CT * T),
        "mask": chunks(a["fside_SxS2_0"]),
        "pad": np.broadcast_to(np.ascontiguousarray(a["mask_BxS2_bf0"]).view(np.uint32)[:, None, :],
                               (BATCHES, P, T // 4)),
        "wpair": np.concatenate(wpair, 1),
        "cst": cst,
        "sel": sel,
        "bq": a["L0_xattn_bq"].reshape(CD, P).T,
        "bk": a["L0_xattn_bk"].reshape(CD, P).T,
        "bv": np.broadcast_to(a["L0_xattn_bv"], (P, D)),
        "bo": np.broadcast_to(a["L0_xattn_bo"], (P, D)),
        "lb": np.broadcast_to(a["L0_ffn_lb_bias"], (P, NE)),
    }
    arrays = {f"in_{k}": np.ascontiguousarray(v) for k, v in arrays.items()}
    nc = bacc.Bacc("TRN2", target_bir_lowering=False, num_devices=1)
    args = [nc.dram_tensor(k, v.shape, mybir.dt.from_np(v.dtype), kind="ExternalInput").ap() for k, v in arrays.items()]
    args.append(nc.dram_tensor("out_x", (BATCHES, P, CT, D), F32, kind="ExternalOutput").ap())
    build(nc, *args)
    r = run_bass_kernel_spmd(nc, [arrays], core_ids=[0])
    got = r.results[0]["out_x"]
    return np.ascontiguousarray(got.transpose(0, 2, 1, 3).reshape(BATCHES, T, D))
```

```python
from contextlib import ExitStack

import concourse.bass as bass
from concourse import mybir

F32 = mybir.dt.float32
F16 = mybir.dt.float16
U32 = mybir.dt.uint32
U8 = mybir.dt.uint8
ALU = mybir.AluOpType
ACT = mybir.ActivationFunctionType
AX = mybir.AxisListType

P = 128
BATCHES, T, D = 32, 256, 256
CT = T // P
CD = D // P
AH, AD = 8, 128
BH, BD = 16, 16
NE = 8
NX = NE + 1
HID = 256
PAIRS = BH // 2
DEPTH = 4
SLOTS = 4
W_UP = 64.0
R_UP = 4.0
H_UP = R_UP * R_UP
MASKED = -3.0e38
EPS = 1e-5
A_SCALE = 1.0 / float(AD) ** 0.5
B_HALF = 0.5 / float(BD) ** 0.5

WQ0 = 0
WK0 = WQ0 + CD * AH * AD
WV0 = WK0 + CD * AD
XQ0 = WV0 + CD * AD
XK0 = XQ0 + CD * D
XV0 = XK0 + CD * D
WO0 = XV0 + CD * D
XO0 = WO0 + AH * D
W10 = XO0 + CD * D
W20 = W10 + NX * CD * HID
GT0 = W20 + NX * 2 * D
NW = GT0 + CD * NE
ID0, TRI0, PE0, PC0, IO0 = 0, P, P + 256, P + 512, P + 513
NC = IO0 + NE
STAGE = 1024


def order(text):
    entries = [entry.replace("@", ":").split(":") for entry in text.split()]
    return [(step, int(arg), int(lag)) for step, arg, lag in entries]


ORDERS = {name: order(text) for name, text in dict(
    sync="""
        b_load:1@1 b_load:2@1 b_load:3@1 b_load:4@1 a_ln:0@0 b_load:5@1 b_load:6@1 b_split_q:0@0 a_T:0@0
        b_mask:0@0 b_load:7@1 c_f2:8@2 b_load:0@0""",
    gpsimd="""
        a_ln:0@0 c_ln:0@2 b_comb:3@1 b_comb:4@1 b_ln:0@1 b_split_k:0@1 b_res:0@1 a_kv:0@0 b_split_q:0@1
        a_q:0@0 b_comb:5@1 c_f1:0@2 a_q:1@0 c_lo:0@2 a_q:2@0 a_q:3@0 b_comb:6@1 c_f1:1@2 c_lo:1@2 c_f1:2@2
        b_kv:0@0 b_comb:7@1 b_comb:8@1 b_comb:9@1 c_lo:2@2 b_comb:10@1 c_f1:3@2 b_comb:11@1 c_lo:3@2
        c_f1:4@2 c_lo:4@2 b_comb:12@1 b_comb:13@1 b_comb:14@1 c_f1:5@2 c_lo:5@2 c_f1:6@2 b_comb:15@1
        c_lo:6@2 c_f1:7@2 c_lo:7@2 c_f1:8@2 c_lo:8@2 b_comb:0@0 b_comb:1@0 b_comb:2@0""",
    scalar="""
        a_pt:7@1 a_pv:6@1 b_pv:15@2 a_pv:7@1 c_T:0@2 b_kv:0@1 a_T:0@0 b_T:0@1 c_f1:0@2 a_kv:0@0 b_stack:4@1
        b_q:0@1 b_stack:5@1 b_stack:6@1 a_q:0@0 b_stack:7@1 b_stack:0@1 b_stack:1@1 c_sq:0@2 c_gate:0@2
        a_q:1@0 b_stack:2@1 b_stack:3@1 a_q:2@0 c_f1:1@2 c_sq:1@2 b_s:0@1 a_q:3@0 a_s:0@0 c_f1:2@2 b_s:1@1
        b_s:2@1 b_pt:0@1 b_s:3@1 a_s:1@0 b_pt:1@1 c_f1:3@2 b_s:4@1 a_pt:0@0 c_sq:2@2 a_s:2@0 b_pt:2@1
        b_s:5@1 c_f1:4@2 b_s:6@1 a_s:3@0 b_pt:3@1 a_pt:1@0 a_pv:0@0 b_s:7@1 c_sq:3@2 b_pt:4@1 a_s:4@0
        c_f1:5@2 b_s:8@1 c_sq:4@2 b_pt:5@1 b_s:9@1 c_f1:6@2 b_pt:6@1 a_pt:2@0 b_s:10@1 a_pv:1@0 b_pt:7@1
        a_s:5@0 b_s:11@1 b_pv:7@1 a_pt:3@0 a_pv:2@0 b_pt:8@1 c_sq:5@2 b_s:12@1 b_pt:9@1 a_s:6@0 c_f1:7@2
        b_s:13@1 c_sq:6@2 a_pt:4@0 b_pt:10@1 a_pv:3@0 a_s:7@0 c_sq:7@2 b_pt:11@1 a_pt:5@0 b_s:14@1 a_pv:4@0
        b_pt:12@1 b_s:15@1 b_pt:13@1 c_f1:8@2 a_pt:6@0 a_pv:5@0 b_pt:14@1 c_sq:8@2 b_pt:15@1""",
    vector="""
        a_ln:0@0 b_wo:0@2 a_ln:1@0 c_ln:0@2 c_ln:1@2 c_ln:2@2 a_ln:2@0 a_wo:0@1 b_ln:0@1 b_ln:1@1 c_T:0@2
        b_ln:2@1 a_T:0@0 b_kv:0@1 b_T:0@1 a_kv:0@0 b_stack:4@1 b_stack:5@1 a_q:0@0 b_stack:6@1 c_gate:0@2
        b_stack:7@1 c_gate:1@2 a_q:1@0 a_q:2@0 c_gate:2@2 c_gate:3@2 c_gate:4@2 c_gate:5@2 c_gate:6@2
        b_s:0@1 c_gate:7@2 a_q:3@0 a_s:0@0 b_s:1@1 b_r:0@1 c_gate:8@2 b_n:0@1 c_gate:9@2 b_s:2@1 a_s:1@0
        c_gate:10@2 a_r:0@0 b_r:1@1 b_s:3@1 b_r:2@1 b_n:1@1 b_n:2@1 a_n:0@0 b_s:4@1 a_s:2@0 b_r:3@1 c_f2:0@2
        b_s:5@1 a_r:1@0 b_n:3@1 a_n:1@0 c_gate:11@2 b_r:4@1 a_s:3@0 a_r:2@0 b_s:6@1 a_pt:0@0 a_s:4@0 b_n:4@1
        b_s:7@1 c_gate:12@2 b_r:5@1 c_f2:1@2 b_r:6@1 a_n:2@0 b_s:8@1 b_n:5@1 a_r:3@0 a_pt:1@0 b_r:7@1
        b_s:9@1 b_n:6@1 a_pv:0@0 a_n:3@0 c_f2:2@2 a_s:5@0 b_r:8@1 a_r:4@0 b_s:10@1 b_n:7@1 b_n:8@1 b_s:11@1
        b_r:9@1 a_pt:2@0 c_f2:3@2 b_n:9@1 a_pv:1@0 b_r:10@1 b_s:12@1 a_s:6@0 b_n:10@1 b_s:13@1 a_n:4@0
        a_pt:3@0 b_pv:7@1 a_r:5@0 c_f2:4@2 b_r:11@1 a_pv:2@0 b_r:12@1 a_s:7@0 b_s:14@1 a_n:5@0 b_r:13@1
        b_n:11@1 a_pt:4@0 c_f2:5@2 a_pv:3@0 b_n:12@1 a_r:6@0 b_n:13@1 b_s:15@1 a_r:7@0 a_n:6@0 b_r:14@1
        a_pt:5@0 a_pv:4@0 b_n:14@1 c_f2:6@2 a_n:7@0 b_r:15@1 b_n:15@1 a_pt:6@0 a_pv:5@0 c_f2:7@2 b_mask:0@0
        a_pt:7@0 a_pv:6@0 b_pv:15@1 c_f2:8@2 a_pv:7@0""",
    tensor="""
        a_T:0@0 c_f1:0@2 b_T:0@1 a_kv:0@0 b_stack:4@1 b_q:0@1 b_stack:5@1 a_q:0@0 b_stack:6@1 b_stack:7@1
        c_gate:0@2 a_q:1@0 b_stack:0@1 b_stack:1@1 a_q:2@0 b_stack:2@1 b_stack:3@1 c_f1:1@2 b_s:0@1 a_q:3@0
        a_s:0@0 b_s:1@1 c_f1:2@2 a_s:1@0 b_s:2@1 c_f2:0@2 b_s:3@1 b_pt:0@1 a_s:2@0 c_f1:3@2 b_s:4@1 b_pt:1@1
        b_pv:0@1 b_s:5@1 a_pt:0@0 a_s:3@0 b_pt:2@1 c_f1:4@2 b_s:6@1 b_pv:1@1 a_s:4@0 b_pt:3@1 b_s:7@1
        a_pt:1@0 c_f2:1@2 a_pv:0@0 b_s:8@1 b_pv:2@1 c_f1:5@2 b_pt:4@1 b_pv:3@1 b_s:9@1 c_f2:2@2 a_s:5@0
        a_pt:2@0 b_pv:4@1 b_pt:5@1 b_s:10@1 c_f1:6@2 a_pv:1@0 b_pv:5@1 b_pt:6@1 a_s:6@0 b_s:11@1 c_f2:3@2
        b_pv:6@1 b_pt:7@1 b_s:12@1 a_pt:3@0 c_f1:7@2 b_pt:8@1 b_pv:7@1 a_pv:2@0 b_s:13@1 a_s:7@0 c_f2:4@2
        b_pt:9@1 b_s:14@1 b_pv:8@1 a_pt:4@0 a_pv:3@0 c_f2:5@2 b_pt:10@1 b_pv:9@1 b_s:15@1 b_pt:11@1
        b_pv:10@1 a_pt:5@0 c_f1:8@2 b_pv:11@1 b_pt:12@1 a_pv:4@0 c_f2:6@2 b_pt:13@1 b_pv:12@1 a_pt:6@0
        a_pv:5@0 b_pt:14@1 c_f2:7@2 b_pv:13@1 b_pt:15@1 a_pt:7@0 a_pv:6@0 b_pv:14@1 b_pv:15@1 c_f2:8@2
        a_pv:7@0 b_wo:0@1 a_wo:0@0 c_T:0@1 b_kv:0@0""",
).items()}
LAGS = 2


def after(batch, per_batch, n):
    if isinstance(batch, int):
        return max(batch * per_batch + n, 0)
    return batch * per_batch + n


def build(nc, x_d, ctx_d, bias_d, mask_d, pad_d, wpair_d, cst_d, sel_d, bq_d, bk_d, bv_d, bo_d, lb_d, out_d):
    with ExitStack() as ctx:
        def sb(name, shape, dt=F32):
            return ctx.enter_context(nc.sbuf_tensor(name, shape, dt))

        def bank(name):
            return ctx.enter_context(nc.psum_tensor(name, [P, 512], F32))

        def sem(name):
            return ctx.enter_context(nc.semaphore(name))

        wh = sb("w_hi", [P, NW], F16)
        wl = sb("w_lo", [P, NW], F16)
        cst = sb("constants", [P, NC])
        ident = cst[:, ID0:ID0 + P]
        tri = cst[:, TRI0:TRI0 + 256]
        pe_t = cst[:, PE0:PE0 + 256]
        pe_first = cst[:, PC0:PC0 + 1]
        iota = cst[:, IO0:IO0 + NE]
        sel = sb("selectors", [P, 16 * P], F16)
        half_mask = sb("half_mask", [P, CT * T])
        pad = sb("key_padding", [P, T // 4], U32)
        b_mask = sb("b_mask", [P, CT * T])
        bq = sb("bq", [P, CD])
        bq_half = sb("bq_half", [P, CD])
        bk = sb("bk", [P, CD])
        bv = sb("bv", [P, D])
        bo = sb("bo", [P, D])
        lb = sb("lb", [P, NE])
        minus_half = sb("minus_half", [P, CT])
        eps = sb("eps", [P, CT])
        zeros = sb("zeros", [P, T])

        x_ln = sb("x_ln", [P, CT, D])
        x_res = sb("x_res", [P, CT, D])
        x1 = sb("x1", [P, CT, D])
        x1_bo = sb("x1_bo", [P, CT, D])
        x2 = sb("x2", [P, CT, D])
        acc = sb("acc", [P, CT, D])
        ln = {}
        for st in "abc":
            ln[st] = dict(
                stats=sb(f"{st}_stats", [P, CT, 6]), mv=sb(f"{st}_mv", [P, CT, 2]), ve=sb(f"{st}_ve", [P, CT]),
                rstd=sb(f"{st}_rstd", [P, CT]),
                xn=x_ln if st == "a" else sb(f"{st}_xn", [P, CT, D]),
                hi=sb(f"{st}_xT_hi", [P, CD, T], F16), lo=sb(f"{st}_xT_lo", [P, CD, T], F16))
        a_k = sb("a_kT", [P, T])
        a_kh = sb("a_kT_hi", [P, T], F16)
        a_kl = sb("a_kT_lo", [P, T], F16)
        a_vh = sb("a_v_hi", [P, CT, AD], F16)
        a_vl = sb("a_v_lo", [P, CT, AD], F16)
        a_q = sb("a_qT", [P, 2, 2, T])
        a_qh = sb("a_qT_hi", [P, AH, T], F16)
        a_ql = sb("a_qT_lo", [P, AH, T], F16)
        a_t = sb("a_neg_scores", [P, 2, 384])
        a_p = sb("a_probs", [P, DEPTH, 384])
        a_pTh = sb("a_probsT_hi", [P, 2, 384], F16)
        a_pTl = sb("a_probsT_lo", [P, 2, 384], F16)
        a_mx = sb("a_neg_max", [P, 2, CT])
        a_sum = sb("a_sum", [P, DEPTH, CT])
        a_inv = sb("a_inv", [P, DEPTH, CT])
        a_oh = sb("a_oT_hi", [P, AH, T], F16)
        a_ol = sb("a_oT_lo", [P, AH, T], F16)
        ctx_f = sb("ctxT", [P, CD, T])
        ctx_h = sb("ctxT_hi", [P, CD, T], F16)
        ctx_l = sb("ctxT_lo", [P, CD, T], F16)
        b_kf = sb("b_kT", [P, CD, T])
        b_kh = sb("b_kT_hi", [P, CD, T], F16)
        b_kl = sb("b_kT_lo", [P, CD, T], F16)
        b_qf = sb("b_qT", [P, CD, T])
        b_qh = sb("b_qT_hi", [P, CD, T], F16)
        b_ql = sb("b_qT_lo", [P, CD, T], F16)
        q_stack = sb("q_stack", [P, PAIRS, T], F16)
        k_even = sb("k_stack_even", [P, PAIRS, T], F16)
        k_odd = sb("k_stack_odd", [P, PAIRS, T], F16)
        b_v = sb("b_v", [P, CT, BH, 32])
        bias = sb("bias", [P, SLOTS, 2 * CT * T])
        b_t = sb("b_neg_scores", [P, 2, CT, T])
        b_p = sb("b_probs", [P, DEPTH, CT, T])
        b_pT = sb("b_probsT", [P, 2, CT, T])
        b_mx = sb("b_neg_max", [P, 2, CT])
        b_sum = sb("b_sum", [P, DEPTH, CT])
        b_inv = sb("b_inv", [P, DEPTH, CT])
        b_oh = sb("b_oT_hi", [P, CD, T], F16)
        b_ol = sb("b_oT_lo", [P, CD, T], F16)
        c_r = sb("c_relu", [P, 2, 2 * T])
        c_h = sb("c_hidden", [P, 2 * T])
        c_hh = sb("c_hidden_hi", [P, 2, 2 * T], F16)
        c_hl = sb("c_hidden_lo", [P, 2, 2 * T], F16)
        g_lg = sb("g_logits", [P, CT, NE])
        g_sel = sb("g_biased", [P, CT, NE])
        g_top = sb("g_top", [P, CT, 8])
        g_idx = sb("g_idx", [P, CT, 8], U32)
        g_idf = sb("g_idx_f", [P, CT, 2])
        g_m1 = sb("g_mask1", [P, CT, NE])
        g_m2 = sb("g_mask2", [P, CT, NE])
        g_ex = sb("g_exp", [P, CT, NE])
        g_e1 = sb("g_exp1", [P, CT, NE])
        g_sg = sb("g_sigmoid", [P, CT, NE])
        g_w = sb("g_w", [P, CT, NE])
        g_s = sb("g_sum", [P, CT])
        g_s1 = sb("g_sum1", [P, CT])
        g_si = sb("g_inv", [P, CT])
        g_we = sb("g_weights", [P, CT, NE])

        ps_as, ps_apt, ps_am = bank("ps_a_scores"), bank("ps_a_probsT"), bank("ps_a_misc")
        ps_bs, ps_bpt, ps_bm = bank("ps_b_scores"), bank("ps_b_probsT"), bank("ps_b_misc")
        ps_c1, ps_c2 = bank("ps_c_hidden"), bank("ps_c_out")
        ln_bank = {"a": ps_am, "b": ps_bm, "c": ps_c1}

        s_cst = sem("consts_loaded")
        s_stage = [sem(f"stage_loaded{n}") for n in range(SLOTS)]
        s_hi, s_lo, s_sel, s_fix = sem("w_hi_ready"), sem("w_lo_ready"), sem("sel_ready"), sem("pool_setup_ready")
        s_bias = [sem(f"bias_loaded{n}") for n in range(SLOTS)]
        s_xln, s_xres, s_ctx = sem("x_ln_loaded"), sem("x_res_loaded"), sem("ctx_loaded")
        s_out = sem("out_stored")
        s_pad, b_m_ok = sem("pad_loaded"), sem("b_mask_ready")
        s_stat = {st: sem(f"{st}_stats_ready") for st in "abc"}
        s_var = {st: sem(f"{st}_var_ready") for st in "abc"}
        s_ve = {st: sem(f"{st}_var_eps_ready") for st in "abc"}
        s_rstd = {st: sem(f"{st}_rstd_ready") for st in "abc"}
        s_xn = {st: sem(f"{st}_xn_ready") for st in "abc"}
        s_lnT = {st: sem(f"{st}_xT_in_psum") for st in "abc"}
        s_xh = {st: sem(f"{st}_xT_hi_ready") for st in "abc"}
        s_xl = {st: sem(f"{st}_xT_lo_ready") for st in "abc"}
        a_kv_ps, a_kv_ok, a_vl_ok = sem("a_kv_in_psum"), sem("a_kv_ready"), sem("a_v_lo_ready")
        a_kh_ok, a_kl_ok = sem("a_k_hi_ready"), sem("a_k_lo_ready")
        a_q_ps, a_q_ok = sem("a_q_in_psum"), sem("a_q_ready")
        a_qh_ok, a_ql_ok = sem("a_q_hi_ready"), sem("a_q_lo_ready")
        a_s_ps, a_t_ok, a_e_ok = sem("a_scores_in_psum"), sem("a_neg_scores_ready"), sem("a_exp_ready")
        a_i_ok, a_n_ok = sem("a_inv_ready"), sem("a_probs_ready")
        a_pt_ps, a_pth_ok, a_pt_ok = sem("a_probsT_in_psum"), sem("a_probsT_hi_ready"), sem("a_probsT_ready")
        a_pv_ps, a_oh_ok, a_o_ok = sem("a_pv_in_psum"), sem("a_oT_hi_ready"), sem("a_oT_ready")
        a_wo_ps, x1_ok = sem("a_wo_in_psum"), sem("x1_ready")
        b_ch, b_cl = sem("ctx_hi_ready"), sem("ctx_lo_ready")
        b_k_ps, b_kf_ok, b_kh_ok, b_kl_ok = sem("b_k_in_psum"), sem("b_k_ready"), sem("b_k_hi"), sem("b_k_lo")
        b_q_ps, b_qf_ok, b_qh_ok, b_ql_ok = sem("b_q_in_psum"), sem("b_q_ready"), sem("b_q_hi"), sem("b_q_lo")
        b_v_ps, b_v_ok = sem("b_v_in_psum"), sem("b_v_ready")
        b_st_ps = sem("b_stack_in_psum")
        b_qst_ok = sem("b_q_stack_ready")
        b_ke_ok, b_ko_ok = sem("b_k_stack_even_ready"), sem("b_k_stack_odd_ready")
        b_c_ok = sem("b_bias_mask_ready")
        b_s_ps, b_t_ok, b_e_ok = sem("b_scores_in_psum"), sem("b_neg_scores_ready"), sem("b_exp_ready")
        b_i_ok, b_n_ok = sem("b_inv_ready"), sem("b_probs_ready")
        b_pt_ps, b_pt_ok = sem("b_probsT_in_psum"), sem("b_probsT_ready")
        b_pv_ps, b_oh_ok, b_o_ok = sem("b_pv_in_psum"), sem("b_oT_hi_ready"), sem("b_oT_ready")
        b_res_ok, b_wo_ps, x2_ok = sem("x1_bo_ready"), sem("b_wo_in_psum"), sem("x2_ready")
        c_g_ps, c_gd, c_ex = sem("c_logits_in_psum"), sem("c_gate_steps"), sem("c_gate_exp")
        c_f1_ps, c_r_ok, c_sq_ok = sem("c_hidden_in_psum"), sem("c_relu_ready"), sem("c_square_ready")
        c_hh_ok, c_h_ok = sem("c_hidden_hi_ready"), sem("c_hidden_ready")
        c_f2_ps, c_a_ok = sem("c_out_in_psum"), sem("c_acc_ready")
        s_carry = sem("carrier")
        GATE_STEPS = 19

        N_PIECES = (NW + STAGE - 1) // STAGE
        pieces = [(n * STAGE, min(NW, (n + 1) * STAGE)) for n in range(N_PIECES)]
        SEL_PIECES = 2
        A_PIECES = -(-XQ0 // STAGE)
        N_CONST = 7
        FIX = 8

        def carry_waits(eng):
            eng.sem_inc(s_carry, 1)
        NSTG = N_PIECES + SEL_PIECES

        def stage_count(n):
            return 16 * (n // SLOTS + 1)

        def walk(engine, steps, i):
            done = 0
            for name, arg, lag in ORDERS[engine]:
                if isinstance(i, int):
                    if not 0 <= i - lag < BATCHES:
                        continue
                    steps[name](i - lag, arg)
                    if i == 0 and "w_split" in steps and (done or name == "a_T"):
                        steps["w_split"](0, done)
                        done += 1
                else:
                    steps[name](i if lag == 0 else i - lag, arg)

        def iterations(eng, engine, steps):
            for i in range(LAGS + 1):
                walk(engine, steps, i)
            with eng.Fori(LAGS + 1, BATCHES - 1) as i:
                walk(engine, steps, i)
            for i in range(BATCHES - 1, BATCHES + LAGS):
                walk(engine, steps, i)

        block = ctx.enter_context(nc.Block())

        @block.sync
        def _(sp):
            sp.dma_start(cst[:, :], cst_d).then_inc(s_cst, 16)
            sp.dma_start(x_ln[:, :, :], x_d[0]).then_inc(s_xln, 16)
            sp.dma_start(bq[:, :], bq_d).then_inc(s_cst, 16)
            sp.dma_start(bk[:, :], bk_d).then_inc(s_cst, 16)
            sp.dma_start(bv[:, :], bv_d).then_inc(s_cst, 16)
            sp.dma_start(bo[:, :], bo_d).then_inc(s_cst, 16)
            sp.dma_start(lb[:, :], lb_d).then_inc(s_cst, 16)
            sp.dma_start(half_mask[:, :], mask_d).then_inc(s_cst, 16)
            sp.dma_start(ctx_f[:, :, :], ctx_d[0]).then_inc(s_ctx, 16)
            sp.dma_start(pad[:, :], pad_d[0]).then_inc(s_pad, 16)
            for n in range(NSTG):
                slot = n % SLOTS
                if n >= SLOTS:
                    sp.wait_ge(s_lo, n - SLOTS + 1)
                if n < N_PIECES:
                    a, z = pieces[n]
                    sp.dma_start(bias[:, slot, 0:z - a], wpair_d[:, a:z]).then_inc(s_stage[slot], 16)
                else:
                    a = (n - N_PIECES) * STAGE
                    sp.dma_start(bias[:, slot, :], sel_d[:, a:a + STAGE]).then_inc(s_stage[slot], 16)
            sp.wait_ge(s_lo, NSTG)
            for p in range(SLOTS):
                sp.dma_start(bias[:, p, :], bias_d[p]).then_inc(s_bias[p], 16)

            def a_ln(b, _):
                sp.wait_ge(x1_ok, after(b, 1, 0))
                sp.dma_start(x_res[:, :, :], x_d[b]).then_inc(s_xres, 16)

            def a_T(b, _):
                sp.wait_ge(s_lnT["a"], after(b, 1, 1))
                if not (isinstance(b, int) and b == BATCHES - 1):
                    sp.dma_start(x_ln[:, :, :], x_d[b + 1]).then_inc(s_xln, 16)

            def b_load(b, p):
                sp.wait_ge(b_t_ok, after(b, BH, 2 * p + 2))
                q = p + SLOTS
                if q < PAIRS:
                    sp.dma_start(bias[:, p % SLOTS, :], bias_d[b * PAIRS + q]).then_inc(s_bias[p % SLOTS], 16)
                elif not (isinstance(b, int) and b == BATCHES - 1):
                    sp.dma_start(bias[:, p % SLOTS, :], bias_d[b * PAIRS + q]).then_inc(s_bias[p % SLOTS], 16)

            def b_split_q(b, _):
                if not (isinstance(b, int) and b == BATCHES - 1):
                    sp.wait_ge(b_cl, after(b, 1, 1))
                    sp.dma_start(ctx_f[:, :, :], ctx_d[b + 1]).then_inc(s_ctx, 16)

            def b_mask_row(b, _):
                if not (isinstance(b, int) and b == BATCHES - 1):
                    sp.wait_ge(b_m_ok, after(b, 1, 1))
                    sp.dma_start(pad[:, :], pad_d[b + 1]).then_inc(s_pad, 16)

            def c_f2(b, e):
                if e == NX - 1:
                    sp.wait_ge(c_a_ok, after(b, NX, NX))
                    sp.dma_start(out_d[b], acc[:, :, :]).then_inc(s_out, 16)

            iterations(sp, "sync", dict(a_ln=a_ln, a_T=a_T, b_load=b_load, b_split_q=b_split_q,
                                b_mask=b_mask_row, c_f2=c_f2))
            sp.wait_ge(s_out, 16 * BATCHES)

        @block.gpsimd
        def _(gp):
            gp.memset(minus_half[:, :], -0.5).then_inc(s_fix, 1)
            gp.memset(eps[:, :], EPS).then_inc(s_fix, 1)
            gp.memset(zeros[:, :], 0.0).then_inc(s_fix, 1)
            gp.memset(k_even[:, :, :], 0.0).then_inc(s_fix, 1)
            gp.memset(k_odd[:, :, :], 0.0).then_inc(s_fix, 1)
            gp.memset(b_v[:, :, :, :], 0.0).then_inc(s_fix, 1)
            gp.wait_ge(s_cst, 16 * N_CONST)
            gp.tensor_scalar(half_mask[:, :], half_mask[:, :], 0.5, None, ALU.mult).then_inc(s_fix, 1)
            gp.tensor_scalar(bq_half[:, :], bq[:, :], B_HALF, None, ALU.mult).then_inc(s_fix, 1)
            gp.wait_ge(s_fix, FIX)

            def ln_rstd(st):
                def step(b, _):
                    L = ln[st]
                    gp.wait_ge(s_var[st], after(b, 2, 2))
                    gp.tensor_tensor(L["ve"][:, :], L["mv"][:, :, 1], eps[:, :], ALU.add).then_inc(s_ve[st], 1)
                    gp.wait_ge(s_ve[st], after(b, 1, 1))
                    if not isinstance(b, int) or b > 0:
                        gp.wait_ge(s_xn[st], after(b, 2, 0))
                    gp.tensor_tensor(L["rstd"][:, :], L["ve"][:, :], minus_half[:, :], ALU.pow).then_inc(s_rstd[st], 1)
                return step

            def a_kv(b, _):
                gp.wait_ge(a_kh_ok, after(b, 1, 1))
                gp.wait_ge(a_s_ps, after(b, AH, 0))
                gp.tensor_tensor(a_kl[:, :], a_k[:, :], a_kh[:, :], ALU.subtract).then_inc(a_kl_ok, 1)

            def a_q_lo(b, r):
                gp.wait_ge(a_qh_ok, after(b, 4, r + 1))
                gp.wait_ge(a_s_ps, after(b, AH, 2 * r + 2 - AH))
                gp.tensor_tensor(a_ql[:, 2 * r:2 * r + 2, :], a_q[:, r % 2, :, :], a_qh[:, 2 * r:2 * r + 2, :],
                                 ALU.subtract).then_inc(a_ql_ok, 1)

            def b_kv(b, _):
                gp.wait_ge(s_ctx, after(b, 16, 16))
                gp.wait_ge(b_v_ps, after(b, 1, 0))
                for m in range(CD):
                    last = gp.tensor_tensor(ctx_h[:, m, :], ctx_f[:, m, :], zeros[:, :], ALU.add)
                last.then_inc(b_ch, 1)
                gp.wait_ge(b_ch, after(b, 1, 1))
                gp.tensor_tensor(ctx_l[:, :, :], ctx_f[:, :, :], ctx_h[:, :, :], ALU.subtract).then_inc(b_cl, 1)

            def split(src, hi, lo, src_ok, hi_ok, lo_ok, first, last):
                def step(b, _):
                    gp.wait_ge(src_ok, after(b, 2, 2))
                    gp.wait_ge(b_st_ps, after(b, 8, last - 8))
                    for m in range(CD):
                        last_half = gp.tensor_tensor(hi[:, m, :], src[:, m, :], zeros[:, :], ALU.add)
                    last_half.then_inc(hi_ok, 1)
                    gp.wait_ge(hi_ok, after(b, 1, 1))
                    gp.tensor_tensor(lo[:, :, :], src[:, :, :], hi[:, :, :], ALU.subtract).then_inc(lo_ok, 1)
                return step

            def b_comb(b, j):
                p = j // 2
                slot = p % SLOTS
                if j == 0:
                    gp.wait_ge(b_m_ok, after(b, 1, 1))
                if j % 2 == 0:
                    gp.wait_ge(s_bias[slot], after(b, 32, 16 * (p // SLOTS + 1)))
                part = bias[:, slot, (j % 2) * 512:(j % 2) * 512 + 512]
                gp.tensor_tensor(part, part, b_mask[:, :], ALU.add).then_inc(b_c_ok, 1)

            def b_res(b, _):
                gp.wait_ge(x1_ok, after(b, 1, 1))
                gp.wait_ge(x2_ok, after(b, 1, 0))
                for c in range(CT):
                    last = gp.tensor_tensor(x1_bo[:, c, :], x1[:, c, :], bo[:, :], ALU.add)
                last.then_inc(b_res_ok, 1)

            def c_f1(b, e):
                gp.wait_ge(c_r_ok, after(b, NX, e + 1))
                gp.wait_ge(c_h_ok, after(b, NX, e))
                gp.tensor_tensor(c_h[:, :], c_r[:, e % 2, :], c_r[:, e % 2, :], ALU.mult).then_inc(c_sq_ok, 1)

            def c_lo(b, e):
                u = e % 2
                gp.wait_ge(c_sq_ok, after(b, NX, e + 1))
                gp.wait_ge(c_hh_ok, after(b, NX, e + 1))
                gp.wait_ge(c_f2_ps, after(b, NX, e - 1))
                gp.tensor_tensor(c_hl[:, u, :], c_h[:, :], c_hh[:, u, :], ALU.subtract).then_inc(c_h_ok, 1)

            iterations(gp, "gpsimd", dict(a_kv=a_kv, a_q=a_q_lo, a_ln=ln_rstd("a"),
                                          b_ln=ln_rstd("b"), c_ln=ln_rstd("c"), b_kv=b_kv,
                                b_split_k=split(b_kf, b_kh, b_kl, b_kf_ok, b_kh_ok, b_kl_ok, 4, 8),
                                b_split_q=split(b_qf, b_qh, b_ql, b_qf_ok, b_qh_ok, b_ql_ok, 0, 8),
                                b_comb=b_comb, b_res=b_res, c_f1=c_f1, c_lo=c_lo))

        @block.scalar
        def _(act):
            def w_hi(n):
                a, z = pieces[n]
                act.wait_ge(s_stage[n % SLOTS], stage_count(n))
                act.activation(wh[:, a:z], bias[:, n % SLOTS, 0:z - a], ACT.Copy, scale=W_UP).then_inc(s_hi, 1)

            def w_split(_, done):
                for n in range(A_PIECES + 2 * done, min(A_PIECES + 2 * done + 2, N_PIECES)):
                    w_hi(n)

            for n in range(A_PIECES):
                w_hi(n)
            act.wait_ge(s_cst, 16 * N_CONST)
            act.wait_ge(s_fix, FIX)

            def ln_hi(st, free_sem, per_batch):
                def step(b, _):
                    L = ln[st]
                    act.wait_ge(s_lnT[st], after(b, 1, 1))
                    act.wait_ge(free_sem, after(b, per_batch, 0))
                    act.activation(L["hi"][:, :, :], ln_bank[st][:, :].rearrange("p (k t) -> p k t", k=CD),
                                   ACT.Copy).then_inc(s_xh[st], 1)
                return step

            def a_kv(b, _):
                act.wait_ge(a_kv_ps, after(b, 1, 1))
                act.wait_ge(a_kl_ok, after(b, 1, 0))
                act.activation(a_k[:, :], ps_am[:, 0:T], ACT.Identity, bias=pe_first, scale=1.0 / W_UP).then_inc(a_kv_ok, 1)
                act.wait_ge(a_pv_ps, after(b, AH, 0))
                act.activation(a_vh[:, :, :], ps_am[:, T:2 * T].rearrange("p (c d) -> p c d", c=CT), ACT.Copy,
                               scale=1.0 / W_UP).then_inc(a_kv_ok, 1)
                act.wait_ge(a_kv_ok, after(b, 2, 1))
                act.wait_ge(a_s_ps, after(b, AH, 0))
                act.activation(a_kh[:, :], a_k[:, :], ACT.Copy).then_inc(a_kh_ok, 1)

            def a_q_hi(b, r):
                act.wait_ge(a_q_ok, after(b, 4, r + 1))
                act.wait_ge(a_s_ps, after(b, AH, 2 * r + 2 - AH))
                act.activation(a_qh[:, 2 * r:2 * r + 2, :], a_q[:, r % 2, :, :], ACT.Copy).then_inc(a_qh_ok, 1)

            def a_s(b, h):
                u, d = h % 2, h % DEPTH
                act.wait_ge(a_t_ok, after(b, AH, h + 1))
                act.wait_ge(a_pt_ps, after(b, AH, h - DEPTH + 1))
                act.activation(a_p[:, d, 0:128], a_t[:, u, 0:128], ACT.Exp, bias=a_mx[:, u, 0:1], scale=-1.0,
                               accum_out=a_sum[:, d, 0:1])
                act.activation(a_p[:, d, 128:384], a_t[:, u, 128:384], ACT.Exp, bias=a_mx[:, u, 1:2], scale=-1.0,
                               accum_out=a_sum[:, d, 1:2]).then_inc(a_e_ok, 1)

            def a_pt(b, h):
                act.wait_ge(a_pt_ps, after(b, AH, h + 1))
                act.wait_ge(a_pv_ps, after(b, AH, h - 1))
                act.activation(a_pTh[:, h % 2, :], ps_apt[:, 0:384], ACT.Copy).then_inc(a_pth_ok, 1)

            def a_pv(b, h):
                act.wait_ge(a_pv_ps, after(b, AH, h + 1))
                act.wait_ge(a_wo_ps, after(b, 1, 0))
                act.activation(a_oh[:, h, :], ps_am[:, 0:T], ACT.Copy).then_inc(a_oh_ok, 1)

            def b_kv(b, _):
                act.wait_ge(b_k_ps, after(b, 1, 1))
                act.wait_ge(b_kl_ok, after(b, 1, 0))
                for m in range(CD):
                    act.activation(b_kf[:, m, :], ps_bpt[:, m * T:(m + 1) * T], ACT.Identity, bias=bk[:, m:m + 1],
                                   scale=1.0 / W_UP).then_inc(b_kf_ok, 1)

            def b_q(b, _):
                act.wait_ge(b_q_ps, after(b, 1, 1))
                act.wait_ge(b_ql_ok, after(b, 1, 0))
                for m in range(CD):
                    act.activation(b_qf[:, m, :], ps_bm[:, m * T:(m + 1) * T], ACT.Identity, bias=bq_half[:, m:m + 1],
                                   scale=B_HALF / W_UP).then_inc(b_qf_ok, 1)

            def b_stack(b, r):
                src = ps_bpt if r % 2 == 0 else ps_bs
                if r >= 4:
                    q = r - 4
                    act.wait_ge(b_st_ps, after(b, 8, q + 1))
                    act.wait_ge(b_s_ps, after(b, BH, 0))
                    act.activation(k_odd[64:128, 2 * q:2 * q + 2, :],
                                   src[64:128, :].rearrange("p (q t) -> p q t", q=2), ACT.Copy).then_inc(b_ko_ok, 1)
                    return
                act.wait_ge(b_st_ps, after(b, 8, 4 + r + 1))
                act.wait_ge(b_s_ps, after(b, BH, 0))
                act.activation(q_stack[:, 2 * r:2 * r + 2, :], src[:, :].rearrange("p (q t) -> p q t", q=2),
                               ACT.Copy).then_inc(b_qst_ok, 1)

            def b_s(b, j):
                u, d = j % 2, j % DEPTH
                act.wait_ge(b_t_ok, after(b, BH, j + 1))
                act.wait_ge(b_pt_ps, after(b, BH, j - DEPTH + 1))
                act.activation(b_p[:, d, 0, :], b_t[:, u, 0, :], ACT.Exp, bias=b_mx[:, u, 0:1], scale=-1.0,
                               accum_out=b_sum[:, d, 0:1])
                act.activation(b_p[:, d, 1, :], b_t[:, u, 1, :], ACT.Exp, bias=b_mx[:, u, 1:2], scale=-1.0,
                               accum_out=b_sum[:, d, 1:2]).then_inc(b_e_ok, 1)

            def b_pt(b, j):
                act.wait_ge(b_pt_ps, after(b, BH, j + 1))
                act.wait_ge(b_pv_ps, after(b, BH, j - 1))
                act.activation(b_pT[:, j % 2, :, :], ps_bpt[:, :].rearrange("p (c t) -> p c t", c=CT),
                               ACT.Copy).then_inc(b_pt_ok, 1)

            def b_pv(b, j):
                if j % 8 == 7:
                    act.wait_ge(b_pv_ps, after(b, BH, j + 1))
                    act.wait_ge(b_wo_ps, after(b, 1, 0))
                    act.activation(b_oh[:, j // 8, :], ps_bm[:, 0:T], ACT.Copy).then_inc(b_oh_ok, 1)

            def c_gate(b, _):
                act.wait_ge(c_gd, after(b, GATE_STEPS, 1))
                act.wait_ge(c_gd, after(b, GATE_STEPS, 0))
                act.activation(g_ex[:, :, :], g_lg[:, :, :], ACT.Exp, scale=-1.0).then_inc(c_ex, 1)

            def c_f1(b, e):
                act.wait_ge(c_f1_ps, after(b, NX, e + 1))
                act.wait_ge(c_sq_ok, after(b, NX, e - 1))
                act.wait_ge(c_hh_ok, after(b, NX, e - 1))
                act.activation(c_r[:, e % 2, :], ps_c1[:, :], ACT.Relu, scale=R_UP / W_UP).then_inc(c_r_ok, 1)

            def c_sq(b, e):
                act.wait_ge(c_r_ok, after(b, NX, e + 1))
                act.wait_ge(c_f2_ps, after(b, NX, e - 1))
                act.activation(c_hh[:, e % 2, :], c_r[:, e % 2, :], ACT.Square).then_inc(c_hh_ok, 1)

            iterations(act, "scalar", dict(w_split=w_split,
                                           a_T=ln_hi("a", a_q_ps, 4), b_T=ln_hi("b", b_q_ps, 1), c_T=ln_hi("c", c_f1_ps, NX),
                                 a_kv=a_kv, a_q=a_q_hi, a_s=a_s, a_pt=a_pt, a_pv=a_pv, b_kv=b_kv, b_q=b_q, b_stack=b_stack,
                                 b_s=b_s, b_pt=b_pt, b_pv=b_pv, c_gate=c_gate, c_f1=c_f1, c_sq=c_sq))

        @block.vector
        def _(dve):
            def w_lo(n):
                if n < N_PIECES:
                    dve.wait_ge(s_hi, n + 1)
                    a, z = pieces[n]
                    dve.scalar_tensor_tensor(out=wl[:, a:z], in0=bias[:, n % SLOTS, 0:z - a], scalar=W_UP,
                                             in1=wh[:, a:z], op0=ALU.mult, op1=ALU.subtract).then_inc(s_lo, 1)
                else:
                    dve.wait_ge(s_stage[n % SLOTS], stage_count(n))
                    a = (n - N_PIECES) * STAGE
                    dve.tensor_copy(sel[:, a:a + STAGE], bias[:, n % SLOTS, :]).then_inc(s_lo, 1)

            def w_split(_, done):
                if A_PIECES + done < NSTG:
                    w_lo(A_PIECES + done)

            for n in range(A_PIECES):
                w_lo(n)
            dve.wait_ge(s_lo, A_PIECES)
            dve.wait_ge(s_cst, 16 * N_CONST)
            dve.wait_ge(s_fix, FIX)

            def ln_parts(st, x, x_ok, x_count):
                def step(b, part):
                    L = ln[st]
                    if part == 0:
                        dve.wait_ge(x_ok, after(b, x_count, x_count))
                        for c in range(CT):
                            dve.bn_stats(L["stats"][:, c, :], x[:, c, :]).then_inc(s_stat[st], 1)
                    elif part == 1:
                        dve.wait_ge(s_stat[st], after(b, 2, 2))
                        carry_waits(dve)
                        for c in range(CT):
                            dve.bn_aggr(L["mv"][:, c, :], L["stats"][:, c, :]).then_inc(s_var[st], 1)
                    else:
                        dve.wait_ge(s_rstd[st], after(b, 1, 1))
                        dve.wait_ge(s_lnT[st], after(b, 1, 0))
                        for c in range(CT):
                            dve.tensor_scalar(L["xn"][:, c, :], x[:, c, :], L["mv"][:, c, 0:1], L["rstd"][:, c:c + 1],
                                              ALU.subtract, ALU.mult).then_inc(s_xn[st], 1)
                return step

            def ln_lo(st):
                def step(b, _):
                    L = ln[st]
                    dve.wait_ge(s_xh[st], after(b, 1, 1))
                    dve.tensor_tensor(L["lo"][:, :, :], ln_bank[st][:, :].rearrange("p (k t) -> p k t", k=CD),
                                      L["hi"][:, :, :], ALU.subtract).then_inc(s_xl[st], 1)
                return step

            def a_wo(b, _):
                dve.wait_ge(a_wo_ps, after(b, 1, 1))
                dve.wait_ge(s_xres, after(b, 16, 16))
                dve.wait_ge(b_res_ok, after(b, 1, 0))
                dve.scalar_tensor_tensor(out=x1[:, :, :], in0=ps_am[:, :].rearrange("p (c d) -> p c d", c=CT),
                                         scalar=1.0 / W_UP, in1=x_res[:, :, :], op0=ALU.mult,
                                         op1=ALU.add).then_inc(x1_ok, 1)

            def a_kv(b, _):
                dve.wait_ge(a_kv_ok, after(b, 2, 2))
                dve.wait_ge(a_pv_ps, after(b, AH, 0))
                dve.scalar_tensor_tensor(out=a_vl[:, :, :], in0=ps_am[:, T:2 * T].rearrange("p (c d) -> p c d", c=CT),
                                         scalar=1.0 / W_UP, in1=a_vh[:, :, :], op0=ALU.mult,
                                         op1=ALU.subtract).then_inc(a_vl_ok, 1)

            def a_pt(b, h):
                dve.wait_ge(a_pth_ok, after(b, AH, h + 1))
                dve.wait_ge(a_pv_ps, after(b, AH, h - 1))
                dve.tensor_tensor(a_pTl[:, h % 2, :], ps_apt[:, 0:384], a_pTh[:, h % 2, :],
                                  ALU.subtract).then_inc(a_pt_ok, 1)

            def a_pv(b, h):
                dve.wait_ge(a_oh_ok, after(b, AH, h + 1))
                dve.wait_ge(a_wo_ps, after(b, 1, 0))
                dve.tensor_tensor(a_ol[:, h, :], ps_am[:, 0:T], a_oh[:, h, :], ALU.subtract).then_inc(a_o_ok, 1)

            def a_qp(b, r):
                dve.wait_ge(a_q_ps, after(b, 4, r + 1))
                dve.wait_ge(a_ql_ok, after(b, 4, r - 1))
                for n in range(2):
                    last = dve.scalar_tensor_tensor(out=a_q[:, r % 2, n, :], in0=ps_am[:, n * T:(n + 1) * T],
                                                    scalar=1.0 / W_UP, in1=pe_t, op0=ALU.mult, op1=ALU.add)
                last.then_inc(a_q_ok, 1)

            def a_s(b, h):
                u = h % 2
                dve.wait_ge(a_s_ps, after(b, AH, h + 1))
                dve.wait_ge(a_e_ok, after(b, AH, h - 1))
                carry_waits(dve)
                dve.tensor_tensor_reduce(out=a_t[:, u, 0:128], in0=ps_as[:, 0:128], in1=tri[:, 128:256], scale=-A_SCALE,
                                         scalar=3.0e38, op0=ALU.add, op1=ALU.min, accum_out=a_mx[:, u, 0:1])
                dve.tensor_tensor_reduce(out=a_t[:, u, 128:384], in0=ps_as[:, 128:384], in1=tri, scale=-A_SCALE,
                                         scalar=3.0e38, op0=ALU.add, op1=ALU.min,
                                         accum_out=a_mx[:, u, 1:2]).then_inc(a_t_ok, 1)

            def a_r(b, h):
                u = h % DEPTH
                dve.wait_ge(a_e_ok, after(b, AH, h + 1))
                dve.reciprocal(a_inv[:, u, :], a_sum[:, u, :]).then_inc(a_i_ok, 1)

            def a_n(b, h):
                u = h % DEPTH
                dve.wait_ge(a_i_ok, after(b, AH, h + 1))
                dve.tensor_scalar(a_p[:, u, 0:128], a_p[:, u, 0:128], a_inv[:, u, 0:1], None, ALU.mult)
                dve.tensor_scalar(a_p[:, u, 128:384], a_p[:, u, 128:384], a_inv[:, u, 1:2], None,
                                  ALU.mult).then_inc(a_n_ok, 1)

            def b_kv(b, _):
                dve.wait_ge(b_v_ps, after(b, 1, 1))
                dve.wait_ge(b_pv_ps, after(b, BH, 0))
                for c in range(CT):
                    for r in range(2):
                        v = ps_bs[:, c * D:(c + 1) * D].rearrange("p (h r d) -> p r h d", r=2, d=BD)[:, r]
                        last = dve.scalar_tensor_tensor(out=b_v[:, c, r:BH:2, r * BD:(r + 1) * BD], in0=v,
                                                        scalar=1.0 / W_UP, in1=bv[:, :].rearrange(
                                                            "p (h r d) -> p r h d", r=2, d=BD)[:, r],
                                                        op0=ALU.mult, op1=ALU.add)
                    last.then_inc(b_v_ok, 1)

            def b_mask_row(b, _):
                dve.wait_ge(s_pad, after(b, 16, 16))
                dve.wait_ge(b_c_ok, after(b, BH, 0))
                for c in range(CT):
                    last = dve.scalar_tensor_tensor(out=b_mask[:, c * T:(c + 1) * T], in0=pad[:, :].bitcast(U8),
                                                    scalar=MASKED,
                                                    in1=half_mask[:, c * T:(c + 1) * T], op0=ALU.mult, op1=ALU.add)
                last.then_inc(b_m_ok, 1)

            def b_stack(b, r):
                if r < 4:
                    return
                q = r - 4
                src = ps_bpt if r % 2 == 0 else ps_bs
                dve.wait_ge(b_st_ps, after(b, 8, q + 1))
                dve.wait_ge(b_s_ps, after(b, BH, 0))
                dve.tensor_copy(k_even[0:64, 2 * q:2 * q + 2, :],
                                src[0:64, :].rearrange("p (q t) -> p q t", q=2)).then_inc(b_ke_ok, 1)

            def b_s(b, j):
                u = j % 2
                slot = (j // 2) % SLOTS
                dve.wait_ge(b_s_ps, after(b, BH, j + 1))
                dve.wait_ge(b_c_ok, after(b, BH, j + 1))
                dve.wait_ge(b_e_ok, after(b, BH, j - 1))
                carry_waits(dve)
                for c in range(CT):
                    at = (j % 2) * 512 + c * T
                    last = dve.tensor_tensor_reduce(out=b_t[:, u, c, :], in0=ps_bs[:, c * T:(c + 1) * T],
                                                    in1=bias[:, slot, at:at + T], scale=-2.0, scalar=3.0e38,
                                                    op0=ALU.add, op1=ALU.min, accum_out=b_mx[:, u, c:c + 1])
                last.then_inc(b_t_ok, 1)

            def b_r(b, j):
                u = j % DEPTH
                dve.wait_ge(b_e_ok, after(b, BH, j + 1))
                dve.reciprocal(b_inv[:, u, :], b_sum[:, u, :]).then_inc(b_i_ok, 1)

            def b_n(b, j):
                u = j % DEPTH
                dve.wait_ge(b_i_ok, after(b, BH, j + 1))
                for c in range(CT):
                    last = dve.tensor_scalar(b_p[:, u, c, :], b_p[:, u, c, :], b_inv[:, u, c:c + 1], None, ALU.mult)
                last.then_inc(b_n_ok, 1)

            def b_pv(b, j):
                if j % 8 == 7:
                    dve.wait_ge(b_oh_ok, after(b, 2, j // 8 + 1))
                    dve.wait_ge(b_wo_ps, after(b, 1, 0))
                    dve.tensor_tensor(b_ol[:, j // 8, :], ps_bm[:, 0:T], b_oh[:, j // 8, :],
                                      ALU.subtract).then_inc(b_o_ok, 1)

            def b_wo(b, _):
                dve.wait_ge(b_wo_ps, after(b, 1, 1))
                dve.wait_ge(b_res_ok, after(b, 1, 1))
                dve.wait_ge(c_a_ok, after(b, NX, 0))
                dve.scalar_tensor_tensor(out=x2[:, :, :], in0=ps_bm[:, :].rearrange("p (c d) -> p c d", c=CT),
                                         scalar=1.0 / W_UP, in1=x1_bo[:, :, :], op0=ALU.mult,
                                         op1=ALU.add).then_inc(x2_ok, 1)

            def c_gate(b, part):
                G = GATE_STEPS
                if part == 0:
                    dve.wait_ge(c_g_ps, after(b, 1, 1))
                    dve.wait_ge(c_gd, after(b, G, 0))
                    dve.tensor_scalar(g_lg[:, :, :], ps_c2[:, 0:CT * NE].rearrange("p (c e) -> p c e", c=CT),
                                      1.0 / W_UP, None, ALU.mult).then_inc(c_gd, 1)
                elif part == 1:
                    dve.wait_ge(c_gd, after(b, G, 1))
                    for c in range(CT):
                        dve.tensor_tensor(g_sel[:, c, :], g_lg[:, c, :], lb[:, :], ALU.add).then_inc(c_gd, 1)
                elif part == 2:
                    dve.wait_ge(c_gd, after(b, G, 3))
                    carry_waits(dve)
                    for c in range(CT):
                        dve.max(g_top[:, c, :], g_sel[:, c, :]).then_inc(c_gd, 1)
                elif part == 3:
                    dve.wait_ge(c_gd, after(b, G, 5))
                    carry_waits(dve)
                    for c in range(CT):
                        dve.max_index(g_idx[:, c, :], g_top[:, c, :], g_sel[:, c, :]).then_inc(c_gd, 1)
                elif part == 4:
                    dve.wait_ge(c_ex, after(b, 1, 1))
                    dve.tensor_scalar(g_e1[:, :, :], g_ex[:, :, :], 1.0, None, ALU.add).then_inc(c_gd, 1)
                elif part == 5:
                    dve.wait_ge(c_gd, after(b, G, 8))
                    dve.tensor_copy(g_idf[:, :, :], g_idx[:, :, 0:2]).then_inc(c_gd, 1)
                    dve.reciprocal(g_sg[:, :, :], g_e1[:, :, :]).then_inc(c_gd, 1)
                elif part == 6:
                    dve.wait_ge(c_gd, after(b, G, 10))
                    for c in range(CT):
                        dve.tensor_scalar(g_m1[:, c, :], iota, g_idf[:, c, 0:1], None,
                                          ALU.is_equal).then_inc(c_gd, 1)
                elif part == 7:
                    dve.wait_ge(c_gd, after(b, G, 12))
                    for c in range(CT):
                        dve.scalar_tensor_tensor(out=g_m2[:, c, :], in0=iota, scalar=g_idf[:, c, 1:2],
                                                 in1=g_m1[:, c, :], op0=ALU.is_equal, op1=ALU.add).then_inc(c_gd, 1)
                elif part == 8:
                    dve.wait_ge(c_gd, after(b, G, 14))
                    dve.tensor_tensor(g_w[:, :, :], g_m2[:, :, :], g_sg[:, :, :], ALU.mult).then_inc(c_gd, 1)
                elif part == 9:
                    dve.wait_ge(c_gd, after(b, G, 15))
                    dve.reduce_sum(g_s[:, :], g_w[:, :, :], axis=AX.X).then_inc(c_gd, 1)
                elif part == 10:
                    dve.wait_ge(c_gd, after(b, G, 16))
                    dve.tensor_scalar(g_s1[:, :], g_s[:, :], 1e-6, None, ALU.add).then_inc(c_gd, 1)
                elif part == 11:
                    dve.wait_ge(c_gd, after(b, G, 17))
                    dve.reciprocal(g_si[:, :], g_s1[:, :]).then_inc(c_gd, 1)
                else:
                    dve.wait_ge(c_gd, after(b, G, 18))
                    for c in range(CT):
                        last = dve.tensor_scalar(g_we[:, c, :], g_w[:, c, :], g_si[:, c:c + 1], 1.0 / (W_UP * H_UP),
                                                 ALU.mult, ALU.mult)
                    last.then_inc(c_gd, 1)

            def c_f2(b, e):
                dve.wait_ge(c_f2_ps, after(b, NX, e + 1))
                if e == 0:
                    dve.wait_ge(s_out, after(b, 16, 0))
                    dve.scalar_tensor_tensor(out=acc[:, :, :], in0=ps_c2[:, :].rearrange("p (c d) -> p c d", c=CT),
                                             scalar=1.0 / (W_UP * H_UP), in1=x2[:, :, :], op0=ALU.mult,
                                             op1=ALU.add).then_inc(c_a_ok, 1)
                    return
                dve.wait_ge(c_a_ok, after(b, NX, e))
                if e == 1:
                    dve.wait_ge(c_gd, after(b, GATE_STEPS, GATE_STEPS))
                for c in range(CT):
                    last = dve.scalar_tensor_tensor(out=acc[:, c, :], in0=ps_c2[:, c * D:(c + 1) * D],
                                                    scalar=g_we[:, c, e - 1:e], in1=acc[:, c, :],
                                                    op0=ALU.mult, op1=ALU.add)
                last.then_inc(c_a_ok, 1)

            iterations(dve, "vector", dict(w_split=w_split,
                                           a_ln=ln_parts("a", x_ln, s_xln, 16), b_ln=ln_parts("b", x1, x1_ok, 1),
                                 c_ln=ln_parts("c", x2, x2_ok, 1), a_T=ln_lo("a"), b_T=ln_lo("b"), c_T=ln_lo("c"),
                                 a_wo=a_wo, a_kv=a_kv, a_pt=a_pt, a_pv=a_pv, a_q=a_qp, a_s=a_s, a_n=a_n, b_kv=b_kv, b_mask=b_mask_row,
                                 b_stack=b_stack, b_s=b_s, b_n=b_n, a_r=a_r, b_r=b_r,
                                 b_pv=b_pv, b_wo=b_wo, c_gate=c_gate, c_f2=c_f2))

        @block.tensor
        def _(pe):
            pe.wait_ge(s_lo, A_PIECES)
            pe.wait_ge(s_cst, 16 * N_CONST)
            pe.wait_ge(s_fix, FIX)

            def all_weights(b):
                if isinstance(b, int) and b == 0:
                    pe.wait_ge(s_lo, NSTG)

            def pair_product(out, stat, mov, full=False, chunks=CD):
                parts = [("h", "h"), ("h", "l"), ("l", "h")] + ([("l", "l")] if full else [])
                for k in range(chunks):
                    for n, (s, m) in enumerate(parts):
                        last = pe.matmul(out, stat(s, k), mov(m, k), start=(k == 0 and n == 0),
                                         stop=(k == chunks - 1 and n == len(parts) - 1))
                return last

            def w(part, at, width):
                return (wh if part == "h" else wl)[:, at:at + width]

            def tokens(st):
                L = ln[st]
                return lambda part, k, c0=0, n=T: (L["hi"] if part == "h" else L["lo"])[:, k, c0:c0 + n]

            def context(part, k, c0=0, n=T):
                return (ctx_h if part == "h" else ctx_l)[:, k, c0:c0 + n]

            def ln_T(st, free_sem, per_batch):
                def step(b, _):
                    L = ln[st]
                    pe.wait_ge(s_xn[st], after(b, 2, 2))
                    pe.wait_ge(free_sem, after(b, per_batch, 0))
                    for k in range(CD):
                        for c in range(CT):
                            last = pe.transpose(ln_bank[st][:, k * T + c * P:k * T + (c + 1) * P],
                                                L["xn"][:, c, k * P:(k + 1) * P], ident)
                    last.then_inc(s_lnT[st], 1)
                return step

            ta, tb, tc = tokens("a"), tokens("b"), tokens("c")

            def a_kv(b, _):
                pe.wait_ge(s_xl["a"], after(b, 1, 1))
                pair_product(ps_am[:, 0:T], lambda s, k: w(s, WK0 + k * AD, AD), lambda m, k: ta(m, k))
                for c in range(CT):
                    last = pair_product(ps_am[:, T + c * AD:T + (c + 1) * AD], lambda s, k: ta(s, k, c * P, P),
                                        lambda m, k: w(m, WV0 + k * AD, AD))
                last.then_inc(a_kv_ps, 1)

            def a_qp(b, r):
                if r == 0:
                    pe.wait_ge(a_vl_ok, after(b, 1, 1))
                else:
                    pe.wait_ge(a_q_ok, after(b, 4, r))
                for n in range(2):
                    h = 2 * r + n
                    last = pair_product(ps_am[:, n * T:(n + 1) * T],
                                        lambda s, k: w(s, WQ0 + k * AH * AD + h * AD, AD), lambda m, k: ta(m, k))
                last.then_inc(a_q_ps, 1)

            def a_s(b, h):
                if h == 0:
                    pe.wait_ge(a_kl_ok, after(b, 1, 1))
                pe.wait_ge(a_ql_ok, after(b, 4, h // 2 + 1))
                pe.wait_ge(a_t_ok, after(b, AH, h))
                for out, q0, keys in [(ps_as[:, 0:128], 0, P), (ps_as[:, 128:384], P, T)]:
                    for n, (q, k) in enumerate([(a_qh, a_kh), (a_qh, a_kl), (a_ql, a_kh)]):
                        last = pe.matmul(out, q[:, h, q0:q0 + P], k[:, 0:keys], start=(n == 0), stop=(n == 2))
                last.then_inc(a_s_ps, 1)

            def a_pt(b, h):
                u = h % DEPTH
                pe.wait_ge(a_n_ok, after(b, AH, h + 1))
                pe.wait_ge(a_pt_ok, after(b, AH, h))
                pe.transpose(ps_apt[:, 0:128], a_p[:, u, 0:128], ident)
                pe.transpose(ps_apt[:, 128:256], a_p[:, u, 128:256], ident)
                pe.transpose(ps_apt[:, 256:384], a_p[:, u, 256:384], ident).then_inc(a_pt_ps, 1)

            def a_pv(b, h):
                u = h % 2
                pe.wait_ge(a_pt_ok, after(b, AH, h + 1))
                if h == 0:
                    pe.wait_ge(a_q_ok, after(b, 4, 4))
                else:
                    pe.wait_ge(a_o_ok, after(b, AH, h))
                for n, (v, pT) in enumerate([(a_vh, a_pTh), (a_vh, a_pTl), (a_vl, a_pTh)]):
                    pe.matmul(ps_am[:, 0:T], v[:, 0, :], pT[:, u, 0:T], start=(n == 0), stop=False)
                    last = pe.matmul(ps_am[:, P:T], v[:, 1, :], pT[:, u, T:384], start=False, stop=(n == 2))
                last.then_inc(a_pv_ps, 1)

            def a_wo(b, _):
                all_weights(b)
                pe.wait_ge(a_o_ok, after(b, AH, AH))
                for c in range(CT):
                    last = pair_product(ps_am[:, c * D:(c + 1) * D],
                                        lambda s, h: (a_oh if s == "h" else a_ol)[:, h, c * P:(c + 1) * P],
                                        lambda m, h: w(m, WO0 + h * D, D), chunks=AH)
                last.then_inc(a_wo_ps, 1)

            def b_kv(b, _):
                all_weights(b)
                pe.wait_ge(b_cl, after(b, 1, 1))
                pe.wait_ge(b_pt_ok, after(b, BH, 0))
                for m in range(CD):
                    last = pair_product(ps_bpt[:, m * T:(m + 1) * T], lambda s, k: w(s, XK0 + k * D + m * P, P),
                                        lambda mm, k: context(mm, k))
                last.then_inc(b_k_ps, 1)
                pe.wait_ge(b_t_ok, after(b, BH, 0))
                for c in range(CT):
                    last = pair_product(ps_bs[:, c * D:(c + 1) * D], lambda s, k: context(s, k, c * P, P),
                                        lambda mm, k: w(mm, XV0 + k * D, D))
                last.then_inc(b_v_ps, 1)

            def b_q(b, _):
                all_weights(b)
                pe.wait_ge(s_xl["b"], after(b, 1, 1))
                for m in range(CD):
                    last = pair_product(ps_bm[:, m * T:(m + 1) * T], lambda s, k: w(s, XQ0 + k * D + m * P, P),
                                        lambda mm, k: tb(mm, k))
                last.then_inc(b_q_ps, 1)

            def b_stack(b, r):
                dst = ps_bpt if r % 2 == 0 else ps_bs
                q = r % 4
                if r >= 4:
                    pe.wait_ge(b_kl_ok, after(b, 1, 1))
                    if r == 4:
                        pe.wait_ge(b_kf_ok, after(b, 2, 2))
                    elif r == 5:
                        pe.wait_ge(b_v_ok, after(b, 2, 2))
                    else:
                        pe.wait_ge(b_ke_ok, after(b, 4, q - 1))
                        pe.wait_ge(b_ko_ok, after(b, 4, q - 1))
                    hi, lo, at = b_kh, b_kl, 8
                else:
                    pe.wait_ge(b_ql_ok, after(b, 1, 1))
                    if r < 2:
                        pe.wait_ge(b_ke_ok, after(b, 4, r + 3))
                        pe.wait_ge(b_ko_ok, after(b, 4, r + 3))
                    else:
                        pe.wait_ge(b_qst_ok, after(b, 4, r - 1))
                    hi, lo, at = b_qh, b_ql, 0
                for n in range(2):
                    pair = 2 * q + n
                    m, row = pair // 4, pair % 4
                    pe.matmul(dst[:, n * T:(n + 1) * T], sel[:, (at + row) * P:(at + row + 1) * P], hi[:, m, :],
                              start=True, stop=False)
                    last = pe.matmul(dst[:, n * T:(n + 1) * T], sel[:, (at + 4 + row) * P:(at + 5 + row) * P], lo[:, m, :],
                                     start=False, stop=True)
                last.then_inc(b_st_ps, 1)

            def b_s(b, j):
                if j == 0:
                    pe.wait_ge(b_qst_ok, after(b, 4, 4))
                    pe.wait_ge(b_ke_ok, after(b, 4, 4))
                    pe.wait_ge(b_ko_ok, after(b, 4, 4))
                else:
                    pe.wait_ge(b_t_ok, after(b, BH, j))
                k = k_even if j % 2 == 0 else k_odd
                for c in range(CT):
                    last = pe.matmul(ps_bs[:, c * T:(c + 1) * T], q_stack[:, j // 2, c * P:(c + 1) * P], k[:, j // 2, :],
                                     start=True, stop=True)
                last.then_inc(b_s_ps, 1)

            def b_pt(b, j):
                u = j % DEPTH
                pe.wait_ge(b_n_ok, after(b, BH, j + 1))
                if j > 0:
                    pe.wait_ge(b_pt_ok, after(b, BH, j))
                for s in range(CT):
                    for c in range(CT):
                        last = pe.transpose(ps_bpt[:, s * T + c * P:s * T + (c + 1) * P],
                                            b_p[:, u, c, s * P:(s + 1) * P], ident)
                last.then_inc(b_pt_ps, 1)

            def b_pv(b, j):
                u, row = j % 2, 32 * (j % 8 // 2)
                pe.wait_ge(b_pt_ok, after(b, BH, j + 1))
                if j == 0:
                    pe.wait_ge(b_qf_ok, after(b, 2, 2))
                    pe.wait_ge(b_v_ok, after(b, 2, 2))
                elif j % 8 == 0:
                    pe.wait_ge(b_o_ok, after(b, 2, j // 8))
                for s in range(CT):
                    last = pe.matmul(ps_bm[row:row + 32, 0:T], b_v[:, s, j, :], b_pT[:, u, s, :],
                                     start=(s == 0 and j % 2 == 0), stop=(s == CT - 1 and j % 2 == 1))
                last.then_inc(b_pv_ps, 1)

            def b_wo(b, _):
                pe.wait_ge(b_o_ok, after(b, 2, 2))
                for c in range(CT):
                    last = pair_product(ps_bm[:, c * D:(c + 1) * D],
                                        lambda s, g: (b_oh if s == "h" else b_ol)[:, g, c * P:(c + 1) * P],
                                        lambda m, g: w(m, XO0 + g * D, D))
                last.then_inc(b_wo_ps, 1)

            def c_gate(b, _):
                pe.wait_ge(s_xl["c"], after(b, 1, 1))
                pe.wait_ge(c_a_ok, after(b, NX, 0))
                for c in range(CT):
                    last = pair_product(ps_c2[:, c * NE:(c + 1) * NE], lambda s, k: tc(s, k, c * P, P),
                                        lambda m, k: w(m, GT0 + k * NE, NE), full=True)
                last.then_inc(c_g_ps, 1)

            def c_f1(b, e):
                if e == 0:
                    pe.wait_ge(s_xl["c"], after(b, 1, 1))
                else:
                    pe.wait_ge(c_r_ok, after(b, NX, e))
                for m in range(2):
                    last = pair_product(ps_c1[:, m * T:(m + 1) * T],
                                        lambda s, k: w(s, W10 + (e * CD + k) * HID + m * P, P), lambda mm, k: tc(mm, k))
                last.then_inc(c_f1_ps, 1)

            def c_f2(b, e):
                pe.wait_ge(c_h_ok, after(b, NX, e + 1))
                if e == 0:
                    pe.wait_ge(c_gd, after(b, GATE_STEPS, 1))
                else:
                    pe.wait_ge(c_a_ok, after(b, NX, e))
                for c in range(CT):
                    last = pair_product(ps_c2[:, c * D:(c + 1) * D],
                                        lambda s, m: (c_hh if s == "h" else c_hl)[:, e % 2,
                                                                                  m * T + c * P:m * T + (c + 1) * P],
                                        lambda mm, m: w(mm, W20 + (e * 2 + m) * D, D))
                last.then_inc(c_f2_ps, 1)

            iterations(pe, "tensor", dict(a_T=ln_T("a", x1_ok, 1), b_T=ln_T("b", x2_ok, 1), c_T=ln_T("c", c_r_ok, NX),
                                a_kv=a_kv, a_q=a_qp, a_s=a_s, a_pt=a_pt, a_pv=a_pv, a_wo=a_wo, b_kv=b_kv, b_q=b_q,
                                b_stack=b_stack, b_s=b_s, b_pt=b_pt, b_pv=b_pv, b_wo=b_wo, c_gate=c_gate, c_f1=c_f1,
                                c_f2=c_f2))


def constants():
    import numpy as np
    cst = np.zeros((P, NC), np.float32)
    cst[:, ID0:ID0 + P] = np.eye(P, dtype=np.float32)
    cst[:, TRI0 + P:TRI0 + 2 * P] = np.where(np.tril(np.ones((P, P), bool)), 0.0, -1e30)
    pos = np.arange(T, dtype=np.float32)[:, None]
    inv = np.exp(-np.log(np.float32(10000.0)) * (np.arange(0, AD, 2, dtype=np.float32) / np.float32(AD))).astype(np.float32)
    ang = pos * inv[None, :]
    table = np.zeros((T, AD), np.float32)
    table[:, 0::2] = np.sin(ang)
    table[:, 1::2] = np.cos(ang)
    cst[:, PE0:PE0 + T] = table.T
    cst[:, PC0] = table[0]
    cst[:, IO0:IO0 + NE] = np.arange(NE, dtype=np.float32)
    sel = np.zeros((P, 16, P), np.float32)
    for kind, rows in enumerate([(0, 1), (2, 3), (0, 2), (1, 3)]):
        for row in range(4):
            for head in range(2):
                for r in rows:
                    for d in range(BD):
                        sel[32 * row + BD * head + d, 4 * kind + row, 64 * head + BD * r + d] = 1.0
    return cst, sel.reshape(P, 16 * P)


def kernel(**inputs):
    import numpy as np
    import concourse.bacc as bacc
    from concourse.bass_utils import run_bass_kernel_spmd

    a = {k: np.asarray(v) for k, v in inputs.items()}

    def chunks(m):
        return m.reshape(-1, P, m.shape[1]).transpose(1, 0, 2).reshape(P, -1)

    wpair = [chunks(a["L0_attn_Wq"].T), chunks(a["L0_attn_Wk"].T), chunks(a["L0_attn_Wv"].T),
             chunks(a["L0_xattn_Wq"].T), chunks(a["L0_xattn_Wk"].T), chunks(a["L0_xattn_Wv"].T),
             chunks(a["L0_attn_Wo"].T), chunks(a["L0_xattn_Wo"].T), chunks(a["L0_ffn_cfc"].T)]
    wpair += [chunks(a["L0_ffn_w1"][e].T) for e in range(NE)]
    wpair += [chunks(a["L0_ffn_cproj"].T)] + [chunks(a["L0_ffn_w2"][e].T) for e in range(NE)]
    wpair += [chunks(a["L0_ffn_gate_w"].T)]
    cst, sel = constants()

    def rows(m):
        return m.reshape(-1, CT, P, m.shape[-1]).transpose(0, 2, 1, 3)

    arrays = {
        "x": rows(a["x"]),
        "ctx": rows(a["ctx_1024"].transpose(0, 2, 1)),
        "bias": a["fside_Bx16xSxS2_0"].reshape(BATCHES * PAIRS, 2 * CT, P, T).transpose(0, 2, 1, 3).reshape(
            BATCHES * PAIRS, P, 2 * CT * T),
        "mask": chunks(a["fside_SxS2_0"]),
        "pad": np.broadcast_to(np.ascontiguousarray(a["mask_BxS2_bf0"]).view(np.uint32)[:, None, :],
                               (BATCHES, P, T // 4)),
        "wpair": np.concatenate(wpair, 1),
        "cst": cst,
        "sel": sel,
        "bq": a["L0_xattn_bq"].reshape(CD, P).T,
        "bk": a["L0_xattn_bk"].reshape(CD, P).T,
        "bv": np.broadcast_to(a["L0_xattn_bv"], (P, D)),
        "bo": np.broadcast_to(a["L0_xattn_bo"], (P, D)),
        "lb": np.broadcast_to(a["L0_ffn_lb_bias"], (P, NE)),
    }
    arrays = {f"in_{k}": np.ascontiguousarray(v) for k, v in arrays.items()}
    nc = bacc.Bacc("TRN2", target_bir_lowering=False, num_devices=1)
    args = [nc.dram_tensor(k, v.shape, mybir.dt.from_np(v.dtype), kind="ExternalInput").ap() for k, v in arrays.items()]
    args.append(nc.dram_tensor("out_x", (BATCHES, P, CT, D), F32, kind="ExternalOutput").ap())
    build(nc, *args)
    r = run_bass_kernel_spmd(nc, [arrays], core_ids=[0])
    got = r.results[0]["out_x"]
    return np.ascontiguousarray(got.transpose(0, 2, 1, 3).reshape(BATCHES, T, D))
```
